# Optimizing a Trainium2 kernel written in Bass

```python
import numpy as np
import jax
import jax.numpy as jnp

def _softmax(x, axis=-1):
    return jax.nn.softmax(x, axis=axis)

def _gelu(x):
    return jax.nn.gelu(x, approximate=True)

def _silu(x):
    return jax.nn.silu(x)

def _sigmoid(x):
    return jax.nn.sigmoid(x)

def _layernorm(x, axis=-1, eps=1e-05):
    m = jnp.mean(x, axis=axis, keepdims=True)
    v = jnp.var(x, axis=axis, keepdims=True)
    return (x - m) / jnp.sqrt(v + eps)

def _scatter_add(tgt, idx, src, axis=0):
    return tgt.at[idx].add(src)

def _segment_sum(src, seg, n):
    return jax.ops.segment_sum(src, seg, n)
kernel_name = 'mk_seq_preln_d2_jaxref_r8_b4906e'

def setup_inputs(seed: int=0):
    np.random.seed(seed)
    _w = jnp.asarray

    def _L0_attn_setup():
        import jax, jax.numpy as jnp
        import numpy as np
        ROPE_BASE = 10000.0
        ROPE_SCALE = 1.0
        ATTN_SCALE = 0.08838834764831845
        WINDOW = 128
        EPS = 1e-06

        def rms_norm(x, scale):
            var = jnp.mean(jnp.square(x), axis=-1, keepdims=True)
            return x * jax.lax.rsqrt(var + EPS) * scale

        def apply_rope(x, positions):
            H = x.shape[-1]
            frac = jnp.arange(0, H, 2, dtype=jnp.float32) / H
            timescale = ROPE_BASE ** frac
            sinusoid = positions[..., None].astype(jnp.float32) / timescale
            sinusoid = sinusoid / ROPE_SCALE
            sin = jnp.sin(sinusoid)[:, :, None, :]
            cos = jnp.cos(sinusoid)[:, :, None, :]
            x1, x2 = jnp.split(x, 2, axis=-1)
            return jnp.concatenate([x1 * cos - x2 * sin, x2 * cos + x1 * sin], axis=-1).astype(x.dtype)
        key = jax.random.key(seed)
        ks = jax.random.split(key, 4)
        B, T, D, N, K, H = (1, 512, 256, 16, 8, 128)
        return {'x': jax.random.normal(ks[0], (B, T, D), jnp.float32), 'q_kernel': jax.random.normal(ks[1], (N, D, H), jnp.float32) * D ** (-0.5), 'kv_kernel': jax.random.normal(ks[2], (2, K, D, H), jnp.float32) * D ** (-0.5), 'out_kernel': jax.random.normal(ks[3], (N, H, D), jnp.float32) * (N * H) ** (-0.5), 'q_norm_scale': jnp.ones((H,), jnp.float32), 'k_norm_scale': jnp.ones((H,), jnp.float32)}
    _L0_attn_in = _L0_attn_setup()

    def _L0_ffn_setup():
        import jax, jax.numpy as jnp
        import numpy as np

        def _sparsify_2to4(h):
            B, S, I = h.shape
            g = h.reshape(B, S, I // 4, 4)
            a = jnp.abs(g)
            _, idx = jax.lax.top_k(a, 2)
            pos = jnp.arange(4)
            mask = (pos == idx[..., 0:1]) | (pos == idx[..., 1:2])
            return (g * mask.astype(g.dtype)).reshape(B, S, I)
        key = jax.random.key(seed)
        k1, k2, k3, k4 = jax.random.split(key, 4)
        B, S, H, I = (4, 256, 256, 1024)
        x = jax.random.normal(k1, (B, S, H), dtype=jnp.float32)
        w_gate = jax.random.normal(k2, (H, I), dtype=jnp.float32) / np.sqrt(H)
        w_up = jax.random.normal(k3, (H, I), dtype=jnp.float32) / np.sqrt(H)
        w_down = jax.random.normal(k4, (I, H), dtype=jnp.float32) / np.sqrt(I)
        return {'x': x, 'w_gate': w_gate, 'w_up': w_up, 'w_down': w_down}
    _L0_ffn_in = _L0_ffn_setup()

    def _L1_attn_setup():
        import jax, jax.numpy as jnp
        import numpy as np
        key = jax.random.key(seed)
        ks = jax.random.split(key, 5)
        B, S, D = (1, 512, 256)
        H, Dh = (16, 128)
        scale = 1.0 / np.sqrt(D).astype(np.float32)
        return {'x': jax.random.normal(ks[0], (B, S, D), dtype=jnp.float32), 'W_K': jax.random.normal(ks[1], (H, Dh, D), dtype=jnp.float32) * scale, 'W_Q': jax.random.normal(ks[2], (H, Dh, D), dtype=jnp.float32) * scale, 'W_V': jax.random.normal(ks[3], (H, Dh, D), dtype=jnp.float32) * scale, 'W_O': jax.random.normal(ks[4], (D, H * Dh), dtype=jnp.float32) * scale}
    _L1_attn_in = _L1_attn_setup()

    def _L1_ffn_setup():
        import jax, jax.numpy as jnp
        import numpy as np
        B, S, D, H = (4, 256, 256, 1024)

        def fwht(x):
            orig_shape = x.shape
            n = orig_shape[-1]
            x = x.reshape(-1, n)
            h = 1
            while h < n:
                xb = x.reshape(-1, n // (2 * h), 2, h)
                a = xb[:, :, 0, :]
                b = xb[:, :, 1, :]
                x = jnp.stack([a + b, a - b], axis=2).reshape(-1, n)
                h *= 2
            scale = jnp.asarray(1.0 / np.sqrt(n), dtype=x.dtype)
            return (x * scale).reshape(orig_shape)
        key = jax.random.key(seed)
        kx, k1, k2, k3 = jax.random.split(key, 4)
        x = jax.random.normal(kx, (B, S, D), dtype=jnp.float32)
        W1 = jax.random.normal(k1, (H, D), dtype=jnp.float32) * (1.0 / np.sqrt(D))
        W2 = jax.random.normal(k2, (D, H), dtype=jnp.float32) * (1.0 / np.sqrt(H))
        W3 = jax.random.normal(k3, (H, D), dtype=jnp.float32) * (1.0 / np.sqrt(D))
        return {'x': x, 'W1': W1, 'W2': W2, 'W3': W3}
    _L1_ffn_in = _L1_ffn_setup()
    _d = {'L0_attn_x': _L0_attn_in['x'], 'L0_attn_q_kernel': _L0_attn_in['q_kernel'], 'L0_attn_kv_kernel': _L0_attn_in['kv_kernel'], 'L0_attn_out_kernel': _L0_attn_in['out_kernel'], 'L0_attn_q_norm_scale': _L0_attn_in['q_norm_scale'], 'L0_attn_k_norm_scale': _L0_attn_in['k_norm_scale'], 'L0_ffn_w_gate': _L0_ffn_in['w_gate'], 'L0_ffn_w_up': _L0_ffn_in['w_up'], 'L0_ffn_w_down': _L0_ffn_in['w_down'], 'L1_attn_W_K': _L1_attn_in['W_K'], 'L1_attn_W_Q': _L1_attn_in['W_Q'], 'L1_attn_W_V': _L1_attn_in['W_V'], 'L1_attn_W_O': _L1_attn_in['W_O'], 'L1_ffn_W1': _L1_ffn_in['W1'], 'L1_ffn_W2': _L1_ffn_in['W2'], 'L1_ffn_W3': _L1_ffn_in['W3']}
    _x0 = _d['L0_attn_x']
    _d['L0_attn_x'] = jax.random.normal(jax.random.fold_in(jax.random.key(seed), 1), (4, 256, 256), dtype=_x0.dtype)
    del _x0
    return _d

def reference(L0_attn_x, L0_attn_q_kernel, L0_attn_kv_kernel, L0_attn_out_kernel, L0_attn_q_norm_scale, L0_attn_k_norm_scale, L0_ffn_w_gate, L0_ffn_w_up, L0_ffn_w_down, L1_attn_W_K, L1_attn_W_Q, L1_attn_W_V, L1_attn_W_O, L1_ffn_W1, L1_ffn_W2, L1_ffn_W3):

    def _L0_attn_ref(x, q_kernel, kv_kernel, out_kernel, q_norm_scale, k_norm_scale):
        import jax, jax.numpy as jnp
        import numpy as np
        ROPE_BASE = 10000.0
        ROPE_SCALE = 1.0
        ATTN_SCALE = 0.08838834764831845
        WINDOW = 128
        EPS = 1e-06

        def rms_norm(x, scale):
            var = jnp.mean(jnp.square(x), axis=-1, keepdims=True)
            return x * jax.lax.rsqrt(var + EPS) * scale

        def apply_rope(x, positions):
            H = x.shape[-1]
            frac = jnp.arange(0, H, 2, dtype=jnp.float32) / H
            timescale = ROPE_BASE ** frac
            sinusoid = positions[..., None].astype(jnp.float32) / timescale
            sinusoid = sinusoid / ROPE_SCALE
            sin = jnp.sin(sinusoid)[:, :, None, :]
            cos = jnp.cos(sinusoid)[:, :, None, :]
            x1, x2 = jnp.split(x, 2, axis=-1)
            return jnp.concatenate([x1 * cos - x2 * sin, x2 * cos + x1 * sin], axis=-1).astype(x.dtype)
        B, T, D = x.shape
        N, _, H = q_kernel.shape
        K = kv_kernel.shape[1]
        G = N // K
        q = jnp.einsum('btd,ndh->btnh', x, q_kernel)
        kv = jnp.einsum('bsd,ckdh->cbskh', x, kv_kernel)
        k, v = (kv[0], kv[1])
        q = rms_norm(q, q_norm_scale)
        k = rms_norm(k, k_norm_scale)
        positions = jnp.broadcast_to(jnp.arange(T)[None, :], (B, T))
        q = apply_rope(q, positions)
        k = apply_rope(k, positions)
        i = jnp.arange(T)[:, None]
        j = jnp.arange(T)[None, :]
        mask = (j <= i) & (i - j < WINDOW)
        qg = q.reshape(B, T, K, G, H)
        logits = jnp.einsum('btkgh,bskh->bkgts', qg * ATTN_SCALE, k)
        logits = jnp.where(mask[None, None, None], logits, jnp.finfo(logits.dtype).min)
        probs = jax.nn.softmax(logits, axis=-1)
        enc = jnp.einsum('bkgts,bskh->btkgh', probs, v).reshape(B, T, N, H)
        return jnp.einsum('btnh,nhd->btd', enc, out_kernel)

    def _L0_ffn_ref(x, w_gate, w_up, w_down):
        import jax, jax.numpy as jnp
        import numpy as np

        def _sparsify_2to4(h):
            B, S, I = h.shape
            g = h.reshape(B, S, I // 4, 4)
            a = jnp.abs(g)
            _, idx = jax.lax.top_k(a, 2)
            pos = jnp.arange(4)
            mask = (pos == idx[..., 0:1]) | (pos == idx[..., 1:2])
            return (g * mask.astype(g.dtype)).reshape(B, S, I)
        h = jax.nn.silu(jnp.einsum('bsh,hi->bsi', x, w_gate)) * jnp.einsum('bsh,hi->bsi', x, w_up)
        h_sparse = _sparsify_2to4(h)
        return jnp.einsum('bsi,ih->bsh', h_sparse, w_down)

    def _L1_attn_ref(x, W_K, W_Q, W_V, W_O):
        import jax, jax.numpy as jnp
        import numpy as np
        b, pos, d_model = x.shape
        d_head = W_K.shape[1]
        k = jnp.einsum('ihd,bpd->biph', W_K, x)
        q = jnp.einsum('ihd,bpd->biph', W_Q, x)
        v = jnp.einsum('ihd,bpd->biph', W_V, x)
        scores = jnp.einsum('biph,biqh->biqp', k, q)
        mask = jnp.tril(jnp.ones((pos, pos), dtype=x.dtype))
        masked = scores * mask - jnp.float32(10000000000.0) * (1.0 - mask)
        attn = jax.nn.softmax(masked / jnp.sqrt(jnp.float32(d_head)), axis=-1)
        z = jnp.einsum('biqp,biph->biqh', attn, v)
        z_flat = jnp.transpose(z, (0, 2, 1, 3)).reshape(b, pos, -1)
        out = jnp.einsum('df,bqf->bqd', W_O, z_flat)
        return out

    def _L1_ffn_ref(x, W1, W2, W3):
        import jax, jax.numpy as jnp
        import numpy as np
        B, S, D, H = (4, 256, 256, 1024)

        def fwht(x):
            orig_shape = x.shape
            n = orig_shape[-1]
            x = x.reshape(-1, n)
            h = 1
            while h < n:
                xb = x.reshape(-1, n // (2 * h), 2, h)
                a = xb[:, :, 0, :]
                b = xb[:, :, 1, :]
                x = jnp.stack([a + b, a - b], axis=2).reshape(-1, n)
                h *= 2
            scale = jnp.asarray(1.0 / np.sqrt(n), dtype=x.dtype)
            return (x * scale).reshape(orig_shape)
        up_gate = jnp.einsum('bsd,hd->bsh', x, W1)
        up_lin = jnp.einsum('bsd,hd->bsh', x, W3)
        hidden = jax.nn.silu(up_gate) * up_lin
        hidden = fwht(hidden)
        out = jnp.einsum('bsh,dh->bsd', hidden, W2)
        return out
    x = L0_attn_x
    x = x + _L0_attn_ref(_layernorm(x, axis=-1), L0_attn_q_kernel, L0_attn_kv_kernel, L0_attn_out_kernel, L0_attn_q_norm_scale, L0_attn_k_norm_scale)
    x = x + _L0_ffn_ref(_layernorm(x, axis=-1), L0_ffn_w_gate, L0_ffn_w_up, L0_ffn_w_down)
    x = x + _L1_attn_ref(_layernorm(x, axis=-1), L1_attn_W_K, L1_attn_W_Q, L1_attn_W_V, L1_attn_W_O)
    x = x + _L1_ffn_ref(_layernorm(x, axis=-1), L1_ffn_W1, L1_ffn_W2, L1_ffn_W3)
    return x

_drawn_inputs = setup_inputs


def setup_inputs(seed=0):
    import zlib

    import numpy as np

    out = dict(_drawn_inputs(seed))
    spreads = {'L0_attn_q_norm_scale': (1.0, 0.2), 'L0_attn_k_norm_scale': (1.0, 0.2)}
    factors = {}
    for name, (base, spread) in spreads.items():
        noise = np.random.default_rng([zlib.crc32(name.encode()), seed]).standard_normal(out[name].shape)
        drawn = base * np.exp(spread * noise) if base else spread * noise
        out[name] = jnp.asarray(drawn.astype(out[name].dtype))
    for name, factor in factors.items():
        out[name] = (out[name] * factor).astype(out[name].dtype)
    return out
```

```python
from contextlib import ExitStack

import concourse.bass as bass
from concourse import mybir

F32 = mybir.dt.float32
F32R = mybir.dt.float32r
BF16 = mybir.dt.bfloat16
ALU = mybir.AluOpType
ACT = mybir.ActivationFunctionType
AX_X = mybir.AxisListType.X

P = 128
D = 256
NC = D // P
TOK = 1024
TILES = TOK // P
DH = 128
PAIRS = 8
UNITS = 8 * PAIRS
HID = 1024
LN_EPS = 1e-5
RMS_EPS = 1e-6
ATTN_SCALE = 0.08838834764831845
ROPE_BASE = 10000.0
LOW = -3.0e38
MASKED = -1.0e30
WA = (1024, 1536)
WA_FFN = 2048
WB = 512
WB_FFN = 1024
FIRST_SLOT, LOOP_FROM, LOOP_STEP, LOOPS, LAST_SLOT = -5, 11, 16, 3, 70
HI_HI, HI_LO, LO_HI = (0, 0), (0, 1), (1, 0)
PASSES = (HI_HI, HI_LO, LO_HI)


def live(it, c):
    return it is not None or 0 <= c < UNITS


def need(eng, sem, it, c, per=1):
    if it is not None:
        eng.wait_ge(sem, it * (LOOP_STEP * per // 1) + c)
    elif c > 0:
        eng.wait_ge(sem, c)


def need_pairs(eng, sem, it, c, per_pair):
    if it is not None:
        eng.wait_ge(sem, it * (2 * per_pair) + c)
    elif c > 0:
        eng.wait_ge(sem, c)


def build(nc, x_in, wa, wax, wb, wdown0, w2t, consts, scales, out):
    with ExitStack() as ctx:
        def sb(name, shape, dt=F32):
            return ctx.enter_context(nc.sbuf_tensor(name, shape, dt))

        def sem(name):
            return ctx.enter_context(nc.semaphore(name))

        bank = [ctx.enter_context(nc.psum_tensor(f"bank{i}", [P, 512], F32)) for i in range(8)]
        S_BANK, PJ_BANK, TQ_BANK, PT_BANK, O_BANK, OP_BANK = 0, 2, 4, 5, 6, 7

        x = sb("x", [P, TILES, D])
        xT = [sb("xT_hi", [P, NC, TOK], F32R), sb("xT_lo", [P, NC, TOK], F32R)]
        xn = sb("xn", [P, 4, D])
        raw_a = sb("raw_a", [P, 2, 1536])
        raw_b = sb("raw_b", [P, 2, WB_FFN])
        a_w = [[sb(f"a_{part}{s}", [P, WA_FFN], F32R) for part in ("hi", "lo")] for s in range(2)]
        b_w = [[sb(f"b_{part}{s}", [P, WB_FFN], F32R) for part in ("hi", "lo")] for s in range(2)]
        qk = sb("qk", [P, 4, TOK])
        v = sb("v", [P, 2, TILES, 2 * DH])
        enc = [sb("enc_hi", [P, 2, TOK], F32R), sb("enc_lo", [P, 2, TOK], F32R)]
        scores = sb("scores", [P, 2, 384])
        probs = sb("probs", [P, 4, 384])
        probs_t = sb("probs_t", [P, 2, 384])
        rowmax = sb("rowmax", [P, 2, 2])
        negmax = sb("negmax", [P, 2, 2])
        rowsum = sb("rowsum", [P, 4, 2])
        rinv = sb("rinv", [P, 4, 2])
        squares = sb("squares", [P, 384])
        sumsq = sb("sumsq", [P, 2, 3])
        meansq = sb("meansq", [P, 2, 3])
        rms_r = sb("rms_r", [P, TILES, 3])
        rot_a = sb("rot_a", [P, 2, 384])
        rot_b = sb("rot_b", [P, 2, 384])
        cos_t = sb("cos_t", [P, 2, 3, DH])
        sin_t = sb("sin_t", [P, 2, 3, DH])
        cst = sb("cst", [P, 1536])
        scl = sb("scl", [P, 4, DH])
        ident = cst[:, 0:128]
        mask = [cst[:, 256:640], cst[:, 640:1024]]
        cos_c = cst[:, 1024:1280].rearrange("p (i d) -> p i d", i=2)
        sin_c = cst[:, 1280:1536].rearrange("p (i d) -> p i d", i=2)
        had_r = sb("had_r", [P, P], F32R)
        zero = sb("zero", [P, 1])
        neg_half = sb("neg_half", [P, TILES])
        ln_stats = sb("ln_stats", [P, 2, 6])
        ln_mv = sb("ln_mv", [P, TILES, 2])
        ln_ve = sb("ln_ve", [P, TILES])
        ln_r = sb("ln_r", [P, TILES])
        gate = sb("gate", [P, 2, 512])
        hid = qk[:, :, :].rearrange("p (b h) t -> p b (h t)", b=2).rearrange("p b (j t) -> p b j t", j=4)
        mag = v[:, 0, :, :].rearrange("p t d -> p (t d)").rearrange("p (j t) -> p j t", j=4)
        cmp = sb("cmp", [P, 6, 512], BF16)
        cnt = sb("cnt", [P, 2, 512], BF16)
        encf = [e[:, :, :].rearrange("p h t -> p (h t)").rearrange("p (j t) -> p j t", j=4) for e in enc]
        w2_a = sb("w2_a", [P, 8, D])
        w2_b = v[:, 1, :, :]
        w2_s = [sb("w2_hi", [P, 512], F32R), sb("w2_lo", [P, 512], F32R)]

        s_x = [sem(f"x_loaded{i}") for i in range(4)]
        s_cst, s_scl, s_w2 = sem("consts_loaded"), sem("scales_loaded"), sem("w2_loaded")
        s_zero, s_half, s_tab, s_scq, s_hadr = (sem(n) for n in ("zero_set", "half_set", "tables_made", "qscale_made", "had_copied"))
        ln = {n: sem("ln_" + n) for n in ("stats", "mv", "ve", "r", "xn", "turned", "hi", "lo")}
        names = ("scores", "max", "nb", "exp", "rinv", "pnorm", "pt", "ptev", "pv", "ehi", "elo", "op", "opadd",
                 "proj", "vproj", "qkev", "vev", "sq", "ss", "ms", "rp", "rot", "radd", "roped", "tq", "tqev",
                 "a0hi", "a0", "ahi", "a", "bhi", "b")
        at = [{n: sem(f"L{L}_{n}") for n in names} for L in range(2)]
        raw_as = [[sem(f"L{L}_raw_a{s}") for s in range(2)] for L in range(2)]
        raw_bs = [[sem(f"L{L}_raw_b{s}") for s in range(2)] for L in range(2)]
        fnames = ("whi", "w", "gate", "up", "silu", "h", "abs", "cmp", "hs", "hi", "lo", "down", "xadd")
        ff = [{n: sem(f"F{f}_{n}") for n in fnames} for f in range(2)]
        s_bf, s_w2hi, s_w2lo, s_hadmm, s_hadev = (sem(n) for n in ("butterfly", "w2_hi_made", "w2_lo_made", "had_product", "w2_made"))
        s_out = sem("stored")

        def ffn_pieces(f):
            rest, main = WA_FFN - WA[f], WA[f]
            ps = [("x0", "a", 0, main + c, c, 10) for c in range(0, rest, 512)]
            ps += [("a9", "a", 1, c, c, 9) for c in range(0, main, 512)]
            ps += [("x1", "a", 1, main + c, c, 11) for c in range(0, rest, 512)]
            ps += [(f"b{s}", "b", s, c, c, 8 + s) for s in range(2) for c in (0, 512)]
            return ps

        pieces = [ffn_pieces(f) for f in range(2)]

        def pieces_until(f, last):
            return max(i + 1 for i, p in enumerate(pieces[f]) if p[0] == last)

        def ln_dve_stats(dve, st, t):
            i = 8 * st + t
            nc.vector.bn_stats(ln_stats[:, t % 2, :], x[:, t, :]).then_inc(ln["stats"], 1)
            dve.wait_ge(ln["stats"], i + 1)
            nc.vector.bn_aggr(ln_mv[:, t, :], ln_stats[:, t % 2, :]).then_inc(ln["mv"], 1)
            dve.wait_ge(ln["mv"], i + 1)
            nc.vector.tensor_scalar(ln_ve[:, t:t + 1], ln_mv[:, t, 1:2], LN_EPS, None, ALU.add).then_inc(ln["ve"], 1)

        def ln_pool(pool, st, t):
            i = 8 * st + t
            pool.wait_ge(ln["ve"], i + 1)
            nc.gpsimd.tensor_tensor(ln_r[:, t:t + 1], ln_ve[:, t:t + 1], neg_half[:, 0:1], ALU.pow).then_inc(ln["r"], 1)

        def ln_dve_scale(dve, st, t):
            i = 8 * st + t
            dve.wait_ge(ln["r"], i + 1)
            if i >= 4:
                dve.wait_ge(ln["turned"], i - 3)
            nc.vector.tensor_scalar(xn[:, t % 4, :], x[:, t, :], ln_mv[:, t, 0:1], ln_r[:, t:t + 1],
                                    ALU.subtract, ALU.mult).then_inc(ln["xn"], 1)

        def ln_pe(pe, st, t, bk):
            i = 8 * st + t
            pe.wait_ge(ln["xn"], i + 1)
            for c in range(NC):
                mm = pe.transpose(bank[bk][:, c * P:(c + 1) * P], xn[:, t % 4, c * P:(c + 1) * P], ident)
            mm.then_inc(ln["turned"], 1)

        def ln_act(act, st, t, bk):
            i = 8 * st + t
            act.wait_ge(ln["turned"], i + 1)
            src = bank[bk][:, 0:D].rearrange("p (c t) -> p c t", c=NC)
            nc.scalar.copy(xT[0][:, :, t * P:(t + 1) * P], src).then_inc(ln["hi"], 1)

        def ln_dve_lo(dve, st, t, bk):
            i = 8 * st + t
            dve.wait_ge(ln["hi"], i + 1)
            src = bank[bk][:, 0:D].rearrange("p (c t) -> p c t", c=NC)
            nc.vector.tensor_tensor(xT[1][:, :, t * P:(t + 1) * P], src, xT[0][:, :, t * P:(t + 1) * P].bitcast(F32),
                                    ALU.subtract).then_inc(ln["lo"], 1)

        def pe_slot(pe, L, it, c):
            s = at[L]
            if live(it, c):
                u = c % 8
                b, hh = u // 2, u % 2
                need(pe, s["max"], it, 2 * c - 2, 2)
                if L == 0:
                    need(pe, s["tqev"], it, c - hh + 2)
                    q, k = hh, 2
                else:
                    need(pe, s["qkev"], it, c - u + 4 * (b // 2) + 2 * hh + 2)
                    q, k = 2 * hh, 2 * hh + 1
                ps = bank[S_BANK + c % 2]
                t0 = b * D
                pe.matmul(ps[:, 0:128], qk[:, q, t0:t0 + 128], qk[:, k, t0:t0 + 128], start=True, stop=True)
                pe.matmul(ps[:, 128:384], qk[:, q, t0 + 128:t0 + 256], qk[:, k, t0:t0 + 256],
                          start=True, stop=True).then_inc(s["scores"], 1)
            m = c - 6
            if live(it, m):
                t, slot = m % 8, (m // 8) % 2
                need(pe, s["elo"], it, m - t % 2 + 2)
                if t == 0:
                    need_pairs(pe, s["b"], it, 4 * (m // 8 + 1), 4)
                need(pe, s["opadd"], it, m)
                for i, (h, (l, r)) in enumerate([(h, p) for h in range(2) for p in PASSES]):
                    mm = pe.matmul(bank[OP_BANK][:, 0:D], enc[l][:, h, t * P:(t + 1) * P],
                                   b_w[slot][r][:, h * D:(h + 1) * D], start=i == 0, stop=i == 5)
                mm.then_inc(s["op"], 1)
            m = c + 5
            if live(it, m):
                t, slot = m % 8, (m // 8) % 2
                if t == 0:
                    if it is None and m == 0:
                        pe.wait_ge(s["a0"], 1 if L == 0 else 4)
                    else:
                        need_pairs(pe, s["a"], it, 4 * (m // 8), 4)
                if it is None and m < 8:
                    ready = m + 1 if L == 0 else 4 * (m // 4 + 1)
                    pe.wait_ge(ln["lo"], 16 * L + ready)
                ps = bank[PJ_BANK + m % 2]
                if L == 0:
                    need(pe, s["rot"], it, m - 1)
                    for i, (g, (l, r)) in enumerate([(g, p) for g in range(NC) for p in PASSES]):
                        mm = pe.matmul(ps[:, :], xT[l][:, g, t * P:(t + 1) * P], a_w[slot][r][:, g * 512:(g + 1) * 512],
                                       start=i == 0, stop=i == 5)
                else:
                    half, w = t // 4, t % 4
                    need(pe, s["qkev"], it, m - 1)
                    for i, (g, (l, r)) in enumerate([(g, p) for g in range(NC) for p in PASSES]):
                        mm = pe.matmul(ps[:, :], a_w[slot][l][:, g * 768 + w * P:g * 768 + (w + 1) * P],
                                       xT[r][:, g, half * 512:(half + 1) * 512], start=i == 0, stop=i == 5)
                mm.then_inc(s["proj"], 1)
            if L == 1:
                m = c + 5
                if live(it, m):
                    t, slot = m % 8, (m // 8) % 2
                    if it is None and m < 8:
                        pe.wait_ge(ln["lo"], 16 + m + 1)
                    need(pe, s["vev"], it, m)
                    for i, (g, (l, r)) in enumerate([(g, p) for g in range(NC) for p in PASSES]):
                        mm = pe.matmul(bank[TQ_BANK][:, 0:D], xT[l][:, g, t * P:(t + 1) * P],
                                       a_w[slot][r][:, g * 768 + 512:(g + 1) * 768], start=i == 0, stop=i == 5)
                    mm.then_inc(s["vproj"], 1)
            m = c - 2
            if live(it, m):
                need(pe, s["pnorm"], it, 2 * m + 2, 2)
                need(pe, s["ptev"], it, m)
                for j in range(3):
                    mm = pe.transpose(bank[PT_BANK][:, j * P:(j + 1) * P], probs[:, m % 4, j * P:(j + 1) * P], ident)
                mm.then_inc(s["pt"], 1)
            m = c - 3
            if live(it, m):
                u = m % 8
                b, hh = u // 2, u % 2
                vc = 0 if L == 0 else hh * DH
                need(pe, s["ptev"], it, m + 1)
                need(pe, s["vev"], it, m - hh + 2)
                need(pe, s["elo"], it, m)
                pe.matmul(bank[O_BANK][:, 0:256], v[:, m // 8 % 2, 2 * b, vc:vc + DH], probs_t[:, m % 2, 0:256],
                          start=True, stop=False, skip_group_check=True)
                pe.matmul(bank[O_BANK][:, 128:256], v[:, m // 8 % 2, 2 * b + 1, vc:vc + DH], probs_t[:, m % 2, 256:384],
                          start=False, stop=True, skip_group_check=True).then_inc(s["pv"], 1)
            if L == 0:
                m = c + 3
                if live(it, m):
                    need(pe, s["roped"], it, m + 1)
                    need(pe, s["tqev"], it, m)
                    for j in range(3):
                        mm = pe.transpose(bank[TQ_BANK][:, j * P:(j + 1) * P], rot_a[:, m % 2, j * P:(j + 1) * P], ident)
                    mm.then_inc(s["tq"], 1)

        def act_slot(act, L, it, c):
            s = at[L]
            m = c - 3
            if live(it, m):
                need(act, s["pt"], it, m + 1)
                need(act, s["pv"], it, m - 1)
                nc.scalar.copy(probs_t[:, m % 2, :], bank[PT_BANK][:, 0:384]).then_inc(s["ptev"], 1)
            m = c - 4
            if live(it, m):
                u = m % 8
                b, hh = u // 2, u % 2
                need(act, s["pv"], it, m + 1)
                need(act, s["op"], it, m - hh - 6)
                nc.scalar.copy(enc[0][:, hh, b * D:(b + 1) * D], bank[O_BANK][:, 0:D]).then_inc(s["ehi"], 1)
            m = c + 4
            if live(it, m):
                t = m % 8
                need(act, s["proj"], it, m + 1)
                if L == 0:
                    need(act, s["ss"], it, m)
                    nc.scalar.activation(squares[:, :], bank[PJ_BANK + m % 2][:, 0:384], ACT.Square).then_inc(s["sq"], 1)
                    need(act, s["pv"], it, m - t % 2 - 14)
                    nc.scalar.copy(v[:, m // 8 % 2, t, 0:DH], bank[PJ_BANK + m % 2][:, 384:512]).then_inc(s["vev"], 1)
                else:
                    half, w = t // 4, t % 4
                    need(act, s["scores"], it, m - t + 4 * half - 4)
                    nc.scalar.copy(qk[:, w, half * 512:(half + 1) * 512], bank[PJ_BANK + m % 2][:, :]).then_inc(s["qkev"], 1)
            if L == 0:
                m = c + 2
                if live(it, m):
                    t = m % 8
                    need(act, s["tq"], it, m + 1)
                    need(act, s["scores"], it, m - t % 2 - 6)
                    nc.scalar.copy(qk[:, 0:3, t * P:(t + 1) * P],
                                   bank[TQ_BANK][:, 0:384].rearrange("p (a t) -> p a t", a=3)).then_inc(s["tqev"], 1)
            if live(it, c):
                u = c % 8
                b, hh = u // 2, u % 2
                need(act, s["nb"], it, c + 1)
                need(act, s["pt"], it, c - 3)
                for r, (c0, c1) in enumerate(((0, 128), (128, 384))):
                    scale = rms_r[:, 2 * b + r, hh:hh + 1] if L == 0 else float(DH) ** -0.5
                    nc.scalar.activation(probs[:, c % 4, c0:c1], scores[:, c % 2, c0:c1], ACT.Exp,
                                         bias=negmax[:, c % 2, r:r + 1], scale=scale,
                                         accum_out=rowsum[:, c % 4, r:r + 1]).then_inc(s["exp"], 1)

        def dve_slot(dve, L, it, c):
            s = at[L]
            m = c - 1
            if live(it, m):
                need(dve, s["exp"], it, 2 * m + 2, 2)
                nc.vector.reciprocal(rinv[:, m % 4, :], rowsum[:, m % 4, :]).then_inc(s["rinv"], 1)
                need(dve, s["rinv"], it, m + 1)
                for r, (c0, c1) in enumerate(((0, 128), (128, 384))):
                    nc.vector.tensor_scalar(probs[:, m % 4, c0:c1], probs[:, m % 4, c0:c1], rinv[:, m % 4, r:r + 1], None,
                                            ALU.mult).then_inc(s["pnorm"], 1)
            m = c - 7
            if live(it, m):
                t = m % 8
                need(dve, s["op"], it, m + 1)
                nc.vector.tensor_tensor(x[:, t, :], bank[OP_BANK][:, 0:D], x[:, t, :], ALU.add).then_inc(s["opadd"], 1)
            if live(it, c):
                u = c % 8
                b, hh = u // 2, u % 2
                need(dve, s["scores"], it, c + 1)
                need(dve, s["exp"], it, 2 * c - 2, 2)
            m = c - 4
            if live(it, m):
                w = m % 8
                need(dve, s["ehi"], it, m + 1)
                dst = slice((w // 2) * D, (w // 2 + 1) * D)
                nc.vector.tensor_tensor(enc[1][:, w % 2, dst], bank[O_BANK][:, 0:D], enc[0][:, w % 2, dst].bitcast(F32),
                                        ALU.subtract).then_inc(s["elo"], 1)
            if live(it, c):
                for r, (c0, c1) in enumerate(((0, 128), (128, 384))):
                    nc.vector.tensor_tensor_reduce(out=scores[:, c % 2, c0:c1], in0=bank[S_BANK + c % 2][:, c0:c1],
                                                   in1=mask[L][:, c0:c1], scale=1.0, scalar=LOW, op0=ALU.add, op1=ALU.max,
                                                   accum_out=rowmax[:, c % 2, r:r + 1]).then_inc(s["max"], 1)
            if live(it, c):
                need(dve, s["max"], it, 2 * c + 2, 2)
                if L == 0:
                    need(dve, s["rp"], it, c - hh + 2)
                    nc.vector.scalar_tensor_tensor(out=negmax[:, c % 2, :], in0=rowmax[:, c % 2, :], scalar=-1.0,
                                                   in1=rms_r[:, 2 * b:2 * b + 2, hh], op0=ALU.mult,
                                                   op1=ALU.mult).then_inc(s["nb"], 1)
                else:
                    nc.vector.tensor_scalar(negmax[:, c % 2, :], rowmax[:, c % 2, :], -float(DH) ** -0.5, None,
                                            ALU.mult).then_inc(s["nb"], 1)
            m = c + 4
            if live(it, m):
                t = m % 8
                if L == 0:
                    ps = bank[PJ_BANK + m % 2]
                    need(dve, s["sq"], it, m + 1)
                    nc.vector.reduce_sum(sumsq[:, m % 2, :], squares[:, :].rearrange("p (a d) -> p a d", a=3),
                                         AX_X).then_inc(s["ss"], 1)
                    need(dve, s["vev"], it, m + 1)
                    need(dve, s["tq"], it, m - 1)
                    nc.vector.tensor_tensor(rot_a[:, m % 2, :], ps[:, 0:384],
                                            cos_t[:, t % 2, :, :].rearrange("p a d -> p (a d)"), ALU.mult)
                    need(dve, s["ss"], it, m + 1)
                    need(dve, s["rp"], it, m - 1)
                    nc.vector.tensor_scalar(meansq[:, m % 2, :], sumsq[:, m % 2, :], 1.0 / DH, RMS_EPS,
                                            ALU.mult, ALU.add).then_inc(s["ms"], 1)
                    need(dve, s["radd"], it, m - 1)
                    nc.vector.tensor_tensor(
                        rot_b[:, m % 2, :].rearrange("p (a h d) -> p a h d", a=3, h=2),
                        ps[:, 0:384].rearrange("p (a h d) -> p a h d", a=3, h=2)[:, :, ::-1, :],
                        sin_t[:, t % 2, :, :].rearrange("p a (h d) -> p a h d", h=2), ALU.mult).then_inc(s["rot"], 1)
                else:
                    need(dve, s["vproj"], it, m + 1)
                    need(dve, s["pv"], it, m - t % 2 - 14)
                    nc.vector.tensor_copy(v[:, m // 8 % 2, t, :], bank[TQ_BANK][:, 0:D]).then_inc(s["vev"], 1)

        def split(hi, lo, src, eng, s_hi, wait, s_lo):
            nc.gpsimd.tensor_tensor(hi, src, zero[:, 0:1].broadcast_to(list(src.shape)), ALU.add).then_inc(s_hi, 1)
            wait()
            nc.gpsimd.tensor_tensor(lo, src, hi.bitcast(F32), ALU.subtract).then_inc(s_lo, 1)

        def pool_slot(pool, L, it, c):
            s = at[L]
            if L == 0:
                m = c + 3
                if live(it, m):
                    t = m % 8
                    need(pool, s["ms"], it, m + 1)
                    need(pool, s["exp"], it, 2 * (m - t % 2) - 12, 2)
                    nc.gpsimd.tensor_tensor(rms_r[:, t, :], meansq[:, m % 2, :], neg_half[:, 0:3], ALU.pow).then_inc(s["rp"], 1)
                    need(pool, s["rot"], it, m + 1)
                    nc.gpsimd.tensor_tensor(rot_a[:, m % 2, :], rot_a[:, m % 2, :], rot_b[:, m % 2, :],
                                            ALU.add).then_inc(s["radd"], 1)
                    need(pool, s["radd"], it, m + 1)
                    need(pool, s["rp"], it, m + 1)
                    nc.gpsimd.tensor_tensor(rot_a[:, m % 2, 256:384], rot_a[:, m % 2, 256:384],
                                            rms_r[:, t, 2:3].broadcast_to([P, DH]), ALU.mult).then_inc(s["roped"], 1)
            m = c + 5
            if (it is not None or 0 <= m < 64) and m % 2 == 0:
                pair, part = m // 8 + 1, m % 8 // 2
                w, slot = WA[L] // 4, pair % 2
                if part == 0:
                    need_pairs(pool, raw_as[L][slot], it, 16 * (pair // 2 + 1), 8)
                    need(pool, s["proj"], it, 8 * (pair - 1))
                    if L == 1:
                        need(pool, s["vproj"], it, 8 * (pair - 1))
                    if L == 1 and it is None and pair == 1:
                        pool.wait_ge(ff[0]["up"], 16)
                cs = slice(part * w, (part + 1) * w)
                done = 4 * (pair - 1) + part + 1
                split(a_w[slot][0][:, cs], a_w[slot][1][:, cs], raw_a[:, slot, cs], pool, s["ahi"],
                      lambda: need_pairs(pool, s["ahi"], it, done, 4), s["a"])
            m = c - 6
            if (it is not None or -8 <= m < 56) and m % 2 == 0:
                pair, part = m // 8 + 1, m % 8 // 2
                w, slot = WB // 4, pair % 2
                if part == 0:
                    need_pairs(pool, raw_bs[L][slot], it, 16 * (pair // 2 + 1), 8)
                    need(pool, s["op"], it, 8 * (pair - 1))
                    if L == 1 and it is None and pair == 0:
                        pool.wait_ge(ff[0]["down"], 12)
                    if L == 1 and it is None and pair == 1:
                        pool.wait_ge(ff[0]["down"], 16)
                cs = slice(part * w, (part + 1) * w)
                done = 4 * pair + part + 1
                split(b_w[slot][0][:, cs], b_w[slot][1][:, cs], raw_b[:, slot, cs], pool, s["bhi"],
                      lambda: need_pairs(pool, s["bhi"], it, done, 4), s["b"])

        def slots(eng, L, body, tail):
            for c in range(FIRST_SLOT, LOOP_FROM):
                body(eng, L, None, c)
            with eng.Fori(0, LOOPS) as it:
                for j in range(LOOP_STEP):
                    body(eng, L, it, LOOP_FROM + j)
            for c in range(LOOP_FROM + LOOP_STEP * LOOPS, LAST_SLOT + 1):
                body(eng, L, None, c)
                tail(c)

        def pe_gate_up(pe, f, k):
            s, L = ff[f], at[f]
            th, t = k // 2, k % 2
            base = 16 * f + 8
            for j in range(4):
                i = 4 * k + j
                r = i % 3
                if j == 0:
                    pe.wait_ge(ln["lo"], base + 4 * (th + 1))
                    if k < 2:
                        if k == 0:
                            pe.wait_ge(L["a"], 32)
                        pe.wait_ge(s["w"], pieces_until(f, "x0" if t == 0 else "x1"))
                if i >= 3:
                    pe.wait_ge(s["silu"], i - 2)
                    pe.wait_ge(s["h"], i - 2)
                elif i == 0:
                    pe.wait_ge(L["max"], 2 * UNITS)
                elif i == 1:
                    pe.wait_ge(L["rot" if f == 0 else "qkev"], UNITS)
                else:
                    pe.wait_ge(L["ptev"], UNITS)
                    pe.wait_ge(ln["lo"], base + 8)
                for up in range(2):
                    ps = bank[2 * r + up]
                    for q, (g, (l, rr)) in enumerate([(g, p) for g in range(NC) for p in PASSES]):
                        c0 = g * HID + up * 512 + j * P
                        mm = pe.matmul(ps[:, :], a_w[t][l][:, c0:c0 + P], xT[rr][:, g, th * 512:(th + 1) * 512],
                                       start=q == 0, stop=q == 5)
                    mm.then_inc(s["up" if up else "gate"], 1)

        def pe_down(pe, f, k):
            s, L = ff[f], at[f]
            t = k % 2
            for tt in range(4):
                d = 4 * k + tt
                if tt == 0:
                    pe.wait_ge(s["hi"], 4 * k + 4)
                    pe.wait_ge(s["lo"], 4 * k + 4)
                    if k < 2:
                        pe.wait_ge(s["w"], pieces_until(f, f"b{t}"))
                if d == 0:
                    pe.wait_ge(L["elo"], UNITS)
                    pe.wait_ge(L["opadd"], UNITS)
                if d >= 2:
                    pe.wait_ge(s["xadd"], d - 1)
                for q, (j, (l, r)) in enumerate([(j, p) for j in range(4) for p in PASSES]):
                    mm = pe.matmul(bank[6 + d % 2][:, 0:D], encf[l][:, j, tt * P:(tt + 1) * P],
                                   b_w[t][r][:, j * D:(j + 1) * D], start=q == 0, stop=q == 11)
                mm.then_inc(s["down"], 1)

        def pe_ln(pe, f, th):
            for t in range(4 * th, 4 * th + 4):
                pe.wait_ge(ff[f]["xadd"], 8 * (th + 1))
                pe.wait_ge(ln["lo"], 8 * (2 * f + 2) + t - 1)
                ln_pe(pe, 2 * f + 2, t, 6 + t % 2)

        def pe_ffn(pe, f):
            pe_gate_up(pe, f, 0)
            pe_gate_up(pe, f, 1)
            pe_down(pe, f, 0)
            pe_gate_up(pe, f, 2)
            pe_down(pe, f, 1)
            pe_gate_up(pe, f, 3)
            if f == 0:
                pe_ln(pe, f, 0)
                pe.wait_ge(s_hadr, 1)
                pe.wait_ge(ln["lo"], 16 + 4)
                for q in range(4):
                    pe.wait_ge(s_w2lo, q + 1)
                    if q >= 2:
                        pe.wait_ge(s_hadev, q - 1)
                    for r in range(2):
                        mm = pe.matmul(bank[6 + q % 2][:, :], had_r[:, :], w2_s[r][:, :], start=r == 0, stop=r == 1)
                    mm.then_inc(s_hadmm, 1)
                pe.wait_ge(s_hadev, 4)
            pe_down(pe, f, 2)
            pe_down(pe, f, 3)
            if f == 0:
                pe_ln(pe, f, 1)

        def act_silu(act, f, i):
            s = ff[f]
            act.wait_ge(s["gate"], i + 1)
            if i >= 2:
                act.wait_ge(s["h"], i - 1)
            nc.scalar.activation(gate[:, i % 2, :], bank[2 * (i % 3)][:, :], ACT.Silu).then_inc(s["silu"], 1)

        def act_ffn(act, f):
            s = ff[f]
            act_silu(act, f, 0)
            act_silu(act, f, 1)
            for k in range(4):
                act_silu(act, f, 4 * k + 2)
                act_silu(act, f, 4 * k + 3)
                if f == 0 and k == 3:
                    for t in range(4):
                        ln_act(act, 2, t, 6 + t % 2)
                    for q in range(4):
                        act.wait_ge(s_hadmm, q + 1)
                        nc.scalar.mul(w2_a[:, 2 * q:2 * q + 2, :].rearrange("p a d -> p (a d)"), bank[6 + q % 2][:, :],
                                      float(HID) ** -0.5).then_inc(s_hadev, 1)
                if f == 0:
                    for j in range(4):
                        act.wait_ge(s["h"], 4 * k + j + 1)
                        if k >= 1:
                            act.wait_ge(s["cmp"], 6 * k)
                        elif j == 0:
                            act.wait_ge(at[0]["pv"], UNITS)
                        nc.scalar.activation(mag[:, j, :], hid[:, k % 2, j, :], ACT.Abs).then_inc(s["abs"], 1)
                if k < 3:
                    act_silu(act, f, 4 * k + 4)
                    act_silu(act, f, 4 * k + 5)
                for j in range(4):
                    act.wait_ge(s["hs" if f == 0 else "h"], 4 * k + j + 1)
                    if j == 0:
                        if k == 0:
                            act.wait_ge(at[f]["op"], UNITS)
                        else:
                            act.wait_ge(s["down"], 4 * k)
                    nc.scalar.copy(encf[0][:, j, :], hid[:, k % 2, j, :]).then_inc(s["hi"], 1)
            if f == 0:
                for t in range(4, 8):
                    ln_act(act, 2, t, 6 + t % 2)

        def dve_hidden(dve, f, i):
            s = ff[f]
            k, j = i // 4, i % 4
            dve.wait_ge(s["silu"], i + 1)
            dve.wait_ge(s["up"], i + 1)
            if i == 0:
                dve.wait_ge(at[f]["scores"], UNITS)
            if k >= 2:
                dve.wait_ge(s["hi"], 4 * k - 4)
                dve.wait_ge(s["lo"], 4 * k - 4)
            nc.vector.tensor_tensor(hid[:, k % 2, j, :], bank[2 * (i % 3) + 1][:, :], gate[:, i % 2, :],
                                    ALU.mult).then_inc(s["h"], 1)

        def dve_xadd(dve, f, k, tt):
            s = ff[f]
            d, t = 4 * k + tt, 4 * (k // 2) + tt
            dve.wait_ge(s["down"], d + 1)
            nc.vector.tensor_tensor(x[:, t, :], bank[6 + d % 2][:, 0:D], x[:, t, :], ALU.add).then_inc(s["xadd"], 1)
            if f == 0 and k % 2 == 1:
                dve.wait_ge(s["xadd"], d + 1)
                ln_dve_stats(dve, 2, t)

        def dve_compare(dve, k, n):
            s = ff[0]
            a, b = ((0, 1), (0, 2), (0, 3), (1, 2), (1, 3), (2, 3))[n]
            dve.wait_ge(s["abs"], 4 * k + b + 1)
            nc.vector.tensor_tensor(cmp[:, n, :], mag[:, a, :], mag[:, b, :], ALU.is_ge).then_inc(s["cmp"], 1)

        def dve_keep(dve, k, chain):
            s = ff[0]
            C01, C02, C03, C12, C13, C23 = range(6)
            rules = ((C01, C02, C03, ALU.add, ALU.is_ge, 1.5), (C12, C13, C01, ALU.subtract, ALU.is_ge, 0.5),
                     (C02, C12, C23, ALU.subtract, ALU.is_lt, 0.5), (C03, C13, C23, ALU.add, ALU.is_lt, 1.5))
            dve.wait_ge(s["cmp"], 6 * k + 6)
            for j, (a, b, c, op, keep, than) in enumerate(rules):
                nc.vector.tensor_tensor(cnt[:, j % 2, :], cmp[:, a, :], cmp[:, b, :], ALU.add).then_inc(chain, 1)
                dve.wait_ge(chain, 8 * k + 2 * j + 1)
                nc.vector.tensor_tensor(cnt[:, j % 2, :], cnt[:, j % 2, :], cmp[:, c, :], op).then_inc(chain, 1)
                dve.wait_ge(chain, 8 * k + 2 * j + 2)
                h = hid[:, k % 2, j, :]
                nc.vector.scalar_tensor_tensor(out=h, in0=cnt[:, j % 2, :], scalar=than, in1=h, op0=keep,
                                               op1=ALU.mult).then_inc(s["hs"], 1)

        s_cnt = sem("kept_counts")

        def dve_ln_rest(dve, th):
            for t in range(4 * th, 4 * th + 4):
                ln_dve_scale(dve, 2, t)
            for t in range(4 * th, 4 * th + 4):
                ln_dve_lo(dve, 2, t, 6 + t % 2)

        def dve_ffn(dve, f):
            s = ff[f]
            dve_hidden(dve, f, 0)
            dve_hidden(dve, f, 1)
            for k in range(4):
                dve_hidden(dve, f, 4 * k + 2)
                dve_hidden(dve, f, 4 * k + 3)
                if f == 0 and k == 3:
                    for t in range(4):
                        ln_dve_lo(dve, 2, t, 6 + t % 2)
                for n in range(6):
                    if f == 0:
                        dve_compare(dve, k, n)
                    if n >= 2 and k >= 1:
                        dve_xadd(dve, f, k - 1, n - 2)
                if f == 0 and k == 2:
                    for t in range(4):
                        ln_dve_scale(dve, 2, t)
                if k < 3:
                    dve_hidden(dve, f, 4 * k + 4)
                    dve_hidden(dve, f, 4 * k + 5)
                if f == 0:
                    dve_keep(dve, k, s_cnt)
                else:
                    for j in range(4):
                        dve.wait_ge(s["hi"], 4 * k + j + 1)
                        nc.vector.tensor_tensor(encf[1][:, j, :], hid[:, k % 2, j, :], encf[0][:, j, :].bitcast(F32),
                                                ALU.subtract).then_inc(s["lo"], 1)
            for tt in range(4):
                dve_xadd(dve, f, 3, tt)
            if f == 0:
                dve_ln_rest(dve, 1)

        def pool_piece(pool, f, n):
            what, ring, slot, col, src, load = pieces[f][n]
            s, L = ff[f], at[f]
            if ring == "a":
                pool.wait_ge(raw_as[f][slot], 16 * (load // 2 + 1))
                if what == "a9":
                    pool.wait_ge(L["proj"], UNITS)
                    if f == 1:
                        pool.wait_ge(L["vproj"], UNITS)
                source, dst = raw_a[:, slot, src:src + 512], a_w[slot]
            else:
                pool.wait_ge(L["op"], UNITS - 8 * (1 - slot))
                if f == 0:
                    pool.wait_ge(raw_bs[0][slot], 16 * (load // 2 + 1))
                    source = raw_b[:, slot, src:src + 512]
                else:
                    pool.wait_ge(s_hadev, 4)
                    a = 4 * slot + src // D
                    source = w2_a[:, a:a + 2, :].rearrange("p a d -> p (a d)")
                dst = b_w[slot]
            split(dst[0][:, col:col + 512], dst[1][:, col:col + 512], source, pool, s["whi"],
                  lambda: pool.wait_ge(s["whi"], n + 1), s["w"])

        def pool_tail(pool, f):
            def tail(c):
                n = c - (LOOP_FROM + LOOP_STEP * LOOPS)
                if n < 5:
                    pool_piece(pool, f, n)
                if 7 <= c - (UNITS - 8) <= 14:
                    ln_pool(pool, 2 * f + 1, c - (UNITS - 8) - 7)
            return tail

        def pool_lo(pool, k):
            s = ff[0]
            for j in range(4):
                pool.wait_ge(s["hi"], 4 * k + j + 1)
                pool.wait_ge(s["down"], 4 * k) if k else pool.wait_ge(at[0]["op"], UNITS)
                nc.gpsimd.tensor_tensor(encf[1][:, j, :], hid[:, k % 2, j, :], encf[0][:, j, :].bitcast(F32),
                                        ALU.subtract).then_inc(s["lo"], 1)

        block = ctx.enter_context(nc.Block())
        last_op = UNITS - 8

        @block.sync
        def _(sp):
            x_v = x_in.rearrange("(t p) d -> p t d", p=P)
            for i in range(4):
                sp.dma_start(x[:, 2 * i:2 * i + 2, :], x_v[:, 2 * i:2 * i + 2, :]).then_inc(s_x[i], 16)
            sp.dma_start(w2_a[:, :, :].rearrange("p a d -> p (a d)"), w2t).then_inc(s_w2, 16)
            for L in range(2):
                s = at[L]

                def load(it, pair):
                    slot = pair % 2
                    if L == 1 and it is None and pair < 2:
                        sp.wait_ge(ff[0]["w"], pieces_until(0, f"x{pair}"))
                        sp.wait_ge(ff[0]["w"], pieces_until(0, f"b{pair}"))
                    if it is None and pair == 2:
                        sp.wait_ge(s["a0"], 1 if L == 0 else 4)
                    else:
                        need_pairs(sp, s["a"], it, 4 * (pair - 2), 4)
                    n = pair if it is None else it * 2 + pair
                    if not (L == 0 and it is None and pair == 0):
                        sp.dma_start(raw_a[:, slot, 0:WA[L]], wa[L][n]).then_inc(raw_as[L][slot], 16)
                    if it is not None or pair < PAIRS:
                        need_pairs(sp, s["b"], it, 4 * (pair - 1), 4)
                        sp.dma_start(raw_b[:, slot, 0:WB], wb[L][n]).then_inc(raw_bs[L][slot], 16)

                for pair in range(4):
                    load(None, pair)
                with sp.Fori(0, 2) as it:
                    load(it, 4)
                    load(it, 5)
                load(None, 8)
                load(None, 9)
                rest = WA_FFN - WA[L]
                sp.wait_ge(s["a"], 32)
                sp.dma_start(raw_a[:, 0, 0:rest], wax[L][0]).then_inc(raw_as[L][0], 16)
                if L == 0:
                    for h in range(2):
                        sp.wait_ge(s["b"], 28 + 4 * h)
                        sp.dma_start(raw_b[:, h, :], wdown0[h]).then_inc(raw_bs[0][h], 16)
                sp.wait_ge(ff[L]["w"], pieces_until(L, "a9"))
                sp.dma_start(raw_a[:, 1, 0:rest], wax[L][1]).then_inc(raw_as[L][1], 16)
            o_v = out.rearrange("(t p) d -> p t d", p=P)
            sp.wait_ge(ff[1]["xadd"], 8)
            sp.dma_start(o_v[:, 0:4, :], x[:, 0:4, :]).then_inc(s_out, 16)
            for t in range(4, 8):
                sp.wait_ge(ff[1]["xadd"], 8 + t + 1)
                sp.dma_start(o_v[:, t, :], x[:, t, :]).then_inc(s_out, 16)
            sp.wait_ge(s_out, 5 * 16)

        @block.gpsimd
        def _(pool):
            nc.gpsimd.memset(zero[:, :], 0.0).then_inc(s_zero, 1)
            nc.gpsimd.memset(neg_half[:, :], -0.5).then_inc(s_half, 1)
            pool.wait_ge(s_zero, 1)
            pool.wait_ge(s_half, 1)
            pool.wait_ge(s_cst, 16)
            for t in range(TILES):
                ln_pool(pool, 0, t)
                if t == 1:
                    pool.wait_ge(s_scq, 1)
                    for tab, c, sc in ((cos_t, cos_c, 0), (sin_t, sin_c, 2)):
                        for a in range(3):
                            nc.gpsimd.tensor_tensor(tab[:, :, a, :], c, scl[:, sc + a // 2, :].unsqueeze(1).broadcast_to([P, 2, DH]),
                                                    ALU.mult).then_inc(s_tab, 1)
            nc.gpsimd.tensor_tensor(had_r[:, :], cst[:, 128:256], zero[:, 0:1].broadcast_to([P, P]), ALU.add).then_inc(s_hadr, 1)
            for L in range(2):
                slots(pool, L, pool_slot, pool_tail(pool, L))
                for n in range(5, len(pieces[L])):
                    pool_piece(pool, L, n)
                if L == 1:
                    break
                pool_lo(pool, 0)
                pool.wait_ge(s_w2, 16)
                src, dst, n = w2_a[:, :, :], w2_b, 0
                for h in (4, 2, 1):
                    a = src.rearrange("p (g s h) d -> p g s (h d)", s=2, h=h)
                    b = dst.rearrange("p (g s h) d -> p g s (h d)", s=2, h=h)
                    nc.gpsimd.tensor_tensor(b[:, :, 0, :], a[:, :, 0, :], a[:, :, 1, :], ALU.add).then_inc(s_bf, 1)
                    nc.gpsimd.tensor_tensor(b[:, :, 1, :], a[:, :, 0, :], a[:, :, 1, :], ALU.subtract).then_inc(s_bf, 1)
                    n += 2
                    pool.wait_ge(s_bf, n)
                    src, dst = dst, src
                pool_lo(pool, 1)
                for q in range(4):
                    if q == 0:
                        for t in range(4):
                            ln_pool(pool, 2, t)
                    if q == 1:
                        pool_lo(pool, 2)
                    if q:
                        pool.wait_ge(s_hadmm, q)
                    split(w2_s[0][:, :], w2_s[1][:, :], src[:, 2 * q:2 * q + 2, :].rearrange("p a d -> p (a d)"), pool, s_w2hi,
                          lambda: pool.wait_ge(s_w2hi, q + 1), s_w2lo)
                pool.wait_ge(raw_as[1][0], 16)
                pool.wait_ge(ff[0]["up"], 12)
                w = WA[1] // 4
                for part in range(4):
                    cs = slice(part * w, (part + 1) * w)
                    if part == 3:
                        pool_lo(pool, 3)
                    split(a_w[0][0][:, cs], a_w[0][1][:, cs], raw_a[:, 0, cs], pool, at[1]["a0hi"],
                          lambda: pool.wait_ge(at[1]["a0hi"], part + 1), at[1]["a0"])
                for t in range(4, 8):
                    ln_pool(pool, 2, t)

        @block.scalar
        def _(act):
            act.dma_start(raw_a[:, 0, 0:WA[0]], wa[0][0]).then_inc(raw_as[0][0], 16)
            act.dma_start(cst[:, :], consts).then_inc(s_cst, 16)
            act.dma_start(scl[:, :, :], scales).then_inc(s_scl, 16)
            act.wait_ge(raw_as[0][0], 16)
            nc.scalar.copy(a_w[0][0][:, 0:WA[0]], raw_a[:, 0, 0:WA[0]]).then_inc(at[0]["a0hi"], 1)
            for t in range(TILES):
                ln_act(act, 0, t, 4 + t % 2)
            for L in range(2):
                def tail(c):
                    t = c - last_op - 9
                    if 0 <= t < 8:
                        if t == 0:
                            act.wait_ge(at[L]["proj"], UNITS)
                            if L == 1:
                                act.wait_ge(at[L]["vproj"], UNITS)
                        ln_act(act, 2 * L + 1, t, 4)
                slots(act, L, act_slot, tail)
                tail(LAST_SLOT + 1)
                tail(LAST_SLOT + 2)
                act_ffn(act, L)

        @block.vector
        def _(dve):
            dve.wait_ge(s_scl, 16)
            for n, i in enumerate((0, 2)):
                ins = nc.vector.tensor_scalar(scl[:, i, :], scl[:, i, :], ATTN_SCALE, None, ALU.mult)
            ins.then_inc(s_scq, 1)
            dve.wait_ge(at[0]["a0hi"], 1)
            nc.vector.tensor_tensor(a_w[0][1][:, 0:WA[0]], raw_a[:, 0, 0:WA[0]], a_w[0][0][:, 0:WA[0]].bitcast(F32),
                                    ALU.subtract).then_inc(at[0]["a0"], 1)
            for t in range(TILES + 2):
                if t < TILES:
                    dve.wait_ge(s_x[t // 2], 16)
                    ln_dve_stats(dve, 0, t)
                if 1 <= t <= TILES:
                    ln_dve_scale(dve, 0, t - 1)
                if 2 <= t:
                    ln_dve_lo(dve, 0, t - 2, 4 + t % 2)
            dve.wait_ge(s_tab, 6)
            for L in range(2):
                def tail(c):
                    t = c - last_op - 7
                    if 0 <= t < 8:
                        dve.wait_ge(at[L]["opadd"], last_op + t + 1)
                        ln_dve_stats(dve, 2 * L + 1, t)
                    if 0 <= t - 1 < 8:
                        ln_dve_scale(dve, 2 * L + 1, t - 1)
                    if 0 <= t - 2 < 8:
                        ln_dve_lo(dve, 2 * L + 1, t - 2, 4)
                slots(dve, L, dve_slot, tail)
                tail(LAST_SLOT + 1)
                tail(LAST_SLOT + 2)
                dve_ffn(dve, L)

        @block.tensor
        def _(pe):
            pe.wait_ge(s_cst, 16)
            for t in range(TILES):
                if t >= 2:
                    pe.wait_ge(ln["lo"], t - 1)
                ln_pe(pe, 0, t, 4 + t % 2)
            pe.wait_ge(ln["lo"], TILES)
            for L in range(2):
                def tail(c):
                    t = c - last_op - 8
                    if 0 <= t < 8:
                        if t == 0:
                            pe.wait_ge(at[L]["tqev" if L == 0 else "vev"], UNITS)
                        else:
                            pe.wait_ge(ln["lo"], 8 * (2 * L + 1) + t)
                        ln_pe(pe, 2 * L + 1, t, 4)
                slots(pe, L, pe_slot, tail)
                tail(LAST_SLOT + 1)
                pe_ffn(pe, L)


def shape_constants(np):
    i = np.arange(P)
    ident = np.eye(P, dtype=np.float32)
    had = np.ones((1, 1), np.float32)
    while had.shape[0] < P:
        had = np.block([[had, had], [had, -had]])
    past, window = i[None, :] <= i[:, None], i[None, :] > i[:, None]
    low = np.float32(MASKED)
    tri = np.where(past, np.float32(0), low)
    win = np.where(window, np.float32(0), low)
    mask0 = np.concatenate([tri, win, tri], 1)
    mask1 = np.concatenate([tri, np.zeros((P, P)), tri], 1)
    frac = np.arange(0, DH, 2, dtype=np.float32) / np.float32(DH)
    timescale = (np.float32(ROPE_BASE) ** frac).astype(np.float32)
    angle = np.arange(2 * P, dtype=np.float32)[:, None] / timescale
    cos, sin = np.cos(angle.astype(np.float64)), np.sin(angle.astype(np.float64))
    cos = np.concatenate([cos, cos], 1).reshape(2, P, DH).transpose(1, 0, 2).reshape(P, 2 * DH)
    sin = np.concatenate([-sin, sin], 1).reshape(2, P, DH).transpose(1, 0, 2).reshape(P, 2 * DH)
    return np.concatenate([ident, had, mask0, mask1, cos, sin], 1).astype(np.float32)


def kernel(**inputs):
    import numpy as np
    import concourse.bacc as bacc
    from concourse.bass_utils import run_bass_kernel_spmd

    a = {n: np.asarray(v) for n, v in inputs.items()}

    def rows(w):
        return w.reshape(NC, P, -1).transpose(1, 0, 2)

    q, kv = a["L0_attn_q_kernel"], a["L0_attn_kv_kernel"]
    pairs0 = [rows(np.concatenate([q[2 * p], q[2 * p + 1], kv[0, p], kv[1, p]], 1)).reshape(P, -1) for p in range(PAIRS)]
    wq, wk, wv = (a[f"L1_attn_W_{n}"].transpose(0, 2, 1) for n in "QKV")
    pairs1 = [rows(np.concatenate([wq[2 * p], wk[2 * p], wq[2 * p + 1], wk[2 * p + 1], wv[2 * p], wv[2 * p + 1]], 1))
              .reshape(P, -1) for p in range(PAIRS)]
    def by_four(w):
        return w.reshape(D, 2, P, 4).transpose(0, 1, 3, 2).reshape(D, 2, 4 * P)

    g0, u0 = by_four(a["L0_ffn_w_gate"]), by_four(a["L0_ffn_w_up"])
    g1, u1 = (a[f"L1_ffn_W{n}"].T.reshape(D, 2, 4 * P) for n in (1, 3))
    halves = [[rows(np.concatenate([g[:, t], u[:, t]], 1)).reshape(P, -1) for t in range(2)] for g, u in ((g0, u0), (g1, u1))]
    wa = [np.stack([w[:, :WA[L]] for w in (pairs0, pairs1)[L] + halves[L]]) for L in range(2)]
    wax = [np.stack([w[:, WA[L]:] for w in halves[L]]) for L in range(2)]
    wb0 = a["L0_attn_out_kernel"].reshape(PAIRS, 2, DH, D).transpose(0, 2, 1, 3).reshape(PAIRS, P, -1)
    wb1 = a["L1_attn_W_O"].T.reshape(PAIRS, 2, DH, D).transpose(0, 2, 1, 3).reshape(PAIRS, P, -1)
    down0 = a["L0_ffn_w_down"].reshape(2, P, 4 * D)
    w2t = a["L1_ffn_W2"].T.reshape(8, P, D).transpose(1, 0, 2).reshape(P, -1)
    sq, sk = a["L0_attn_q_norm_scale"], a["L0_attn_k_norm_scale"]
    swap = np.roll(np.arange(DH), DH // 2)
    scales = np.broadcast_to(np.stack([sq, sk, sq[swap], sk[swap]])[None], (P, 4, DH))
    arrays = {
        "x": a["L0_attn_x"].reshape(TOK, D), "wa0": wa[0], "wa1": wa[1], "wax0": wax[0], "wax1": wax[1],
        "wb0": wb0, "wb1": wb1, "wdown0": down0, "w2t": w2t, "consts": shape_constants(np), "scales": scales,
    }
    arrays = {n: np.ascontiguousarray(v) for n, v in arrays.items()}
    nc = bacc.Bacc("TRN2", target_bir_lowering=False, num_devices=1)
    d = {n: nc.dram_tensor(f"in_{n}", v.shape, F32, kind="ExternalInput").ap() for n, v in arrays.items()}
    out = nc.dram_tensor("out", (TOK, D), F32, kind="ExternalOutput").ap()
    build(nc, d["x"], (d["wa0"], d["wa1"]), (d["wax0"], d["wax1"]), (d["wb0"], d["wb1"]), d["wdown0"], d["w2t"],
          d["consts"], d["scales"], out)
    r = run_bass_kernel_spmd(nc, [{f"in_{n}": v for n, v in arrays.items()}], core_ids=[0])
    return r.results[0]["out"].reshape(4, 256, D)
```

```python
from contextlib import ExitStack

import concourse.bass as bass
from concourse import mybir

F32 = mybir.dt.float32
F32R = mybir.dt.float32r
BF16 = mybir.dt.bfloat16
ALU = mybir.AluOpType
ACT = mybir.ActivationFunctionType
AX_X = mybir.AxisListType.X

P = 128
D = 256
NC = D // P
TOK = 1024
TILES = TOK // P
DH = 128
PAIRS = 8
UNITS = 8 * PAIRS
HID = 1024
LN_EPS = 1e-5
RMS_EPS = 1e-6
ATTN_SCALE = 0.08838834764831845
ROPE_BASE = 10000.0
LOW = -3.0e38
MASKED = -1.0e30
WA = (1024, 1536)
WA_FFN = 2048
WB = 512
WB_FFN = 1024
FIRST_SLOT, LOOP_FROM, LOOP_STEP, LOOPS, LAST_SLOT = -5, 11, 16, 3, 70
FIRST_TAIL = UNITS - 8 + 7
TAIL_SLOT = UNITS - 4
HI_HI, HI_LO, LO_HI = (0, 0), (0, 1), (1, 0)
PASSES = (HI_HI, HI_LO, LO_HI)


def live(it, c):
    return it is not None or 0 <= c < UNITS


def need(eng, sem, it, c, per=1):
    if it is not None:
        eng.wait_ge(sem, it * (LOOP_STEP * per) + max(c, 1))
    elif c > 0:
        eng.wait_ge(sem, c)


def need_pairs(eng, sem, it, c, per_pair):
    if it is not None:
        eng.wait_ge(sem, it * (2 * per_pair) + c)
    elif c > 0:
        eng.wait_ge(sem, c)


def build(nc, x_in, wa, wax, wb, wdown0, w2t, consts, scales, out):
    with ExitStack() as ctx:
        def sb(name, shape, dt=F32):
            return ctx.enter_context(nc.sbuf_tensor(name, shape, dt))

        def sem(name):
            return ctx.enter_context(nc.semaphore(name))

        bank = [ctx.enter_context(nc.psum_tensor(f"bank{i}", [P, 512], F32)) for i in range(8)]
        S_BANK, PJ_BANK, TQ_BANK, PT_BANK, O_BANK, OP_BANK = 0, 2, 4, 5, 6, 7

        x = sb("x", [P, TILES, D])
        xT = [sb("xT_hi", [P, NC, TOK], F32R), sb("xT_lo", [P, NC, TOK], F32R)]
        xn = sb("xn", [P, 4, D])
        raw_a = sb("raw_a", [P, 2, 1536])
        raw_b = sb("raw_b", [P, 2, WB_FFN])
        a_w = [[sb(f"a_{part}{s}", [P, WA_FFN], F32R) for part in ("hi", "lo")] for s in range(2)]
        b_w = [[sb(f"b_{part}{s}", [P, WB_FFN], F32R) for part in ("hi", "lo")] for s in range(2)]
        qk = sb("qk", [P, 4, TOK])
        v = sb("v", [P, 2, TILES, 2 * DH])
        enc = [sb("enc_hi", [P, 2, TOK], F32R), sb("enc_lo", [P, 2, TOK], F32R)]
        scores = sb("scores", [P, 2, 384])
        probs = sb("probs", [P, 4, 384])
        probs_t = sb("probs_t", [P, 2, 384])
        rowmax = sb("rowmax", [P, 2, 2])
        negmax = sb("negmax", [P, 2, 2])
        rowsum = sb("rowsum", [P, 4, 2])
        rinv = sb("rinv", [P, 4, 2])
        squares = sb("squares", [P, 384])
        sumsq = sb("sumsq", [P, 2, 3])
        meansq = sb("meansq", [P, 2, 3])
        rms_r = sb("rms_r", [P, TILES, 3])
        rot_a = sb("rot_a", [P, 2, 384])
        rot_b = sb("rot_b", [P, 2, 384])
        cos_t = sb("cos_t", [P, 2, 3, DH])
        sin_t = sb("sin_t", [P, 2, 3, DH])
        cst = sb("cst", [P, 1536])
        scl = sb("scl", [P, 4, DH])
        ident = cst[:, 0:128]
        mask = [cst[:, 768:1152], cst[:, 1152:1536]]
        cos_c = cst[:, 256:512].rearrange("p (i d) -> p i d", i=2)
        sin_c = cst[:, 512:768].rearrange("p (i d) -> p i d", i=2)
        had_r = sb("had_r", [P, P], F32R)
        zero = sb("zero", [P, 1])
        neg_half = sb("neg_half", [P, TILES])
        ln_stats = sb("ln_stats", [P, 2, 6])
        ln_mv = sb("ln_mv", [P, TILES, 2])
        ln_ve = sb("ln_ve", [P, TILES])
        ln_r = sb("ln_r", [P, TILES])
        gate = sb("gate", [P, 2, 512])
        hid = qk[:, :, :].rearrange("p (b h) t -> p b (h t)", b=2).rearrange("p b (j t) -> p b j t", j=4)
        mag = v[:, 0, :, :].rearrange("p t d -> p (t d)").rearrange("p (j t) -> p j t", j=4)
        work = sb("work", [P, 2560])
        bits = work[:, :].bitcast(BF16).rearrange("p (n t) -> p n t", t=512)
        cmp, cnt = bits[:, 0:6, :], bits[:, 6:10, :]
        encf = [e[:, :, :].rearrange("p h t -> p (h t)").rearrange("p (j t) -> p j t", j=4) for e in enc]
        w2_a = sb("w2_a", [P, 8, D])
        w2_b = work[:, 0:8 * D].rearrange("p (a d) -> p a d", d=D)
        w2_s = [sb("w2_hi", [P, 512], F32R), sb("w2_lo", [P, 512], F32R)]

        s_x = [sem(f"x_loaded{i}") for i in range(4)]
        s_ident, s_rope, s_mask = sem("identity_loaded"), sem("rotation_loaded"), sem("masks_loaded")
        s_scl, s_w2 = sem("scales_loaded"), sem("w2_loaded")
        s_zero, s_half, s_tab, s_scq, s_hadr = (sem(n) for n in ("zero_set", "half_set", "tables_made", "qscale_made", "had_copied"))
        ln = {n: sem("ln_" + n) for n in ("stats", "mv", "ve", "r", "xn", "turned", "hi", "lo")}
        names = ("scores", "max", "nb", "exp", "rinv", "pnorm", "pt", "ptev", "pv", "ehi", "elo", "op", "opadd",
                 "proj", "vproj", "qkev", "vev", "sq", "ss", "ms", "rp", "rot", "radd", "roped", "tq", "tqev",
                 "a0hi", "a0", "ahi", "a", "bhi", "b")
        at = [{n: sem(f"L{L}_{n}") for n in names} for L in range(2)]
        raw_as = [[sem(f"L{L}_raw_a{s}") for s in range(2)] for L in range(2)]
        raw_bs = [[sem(f"L{L}_raw_b{s}") for s in range(2)] for L in range(2)]
        fnames = ("whi", "w", "gate", "up", "silu", "h", "abs", "cmp", "hs", "hi", "lo", "lo23", "down", "xadd")
        ff = [{n: sem(f"F{f}_{n}") for n in fnames} for f in range(2)]
        s_bf, s_w2hi, s_w2lo, s_hadmm, s_hadev = (sem(n) for n in ("butterfly", "w2_hi_made", "w2_lo_made", "had_product", "w2_made"))
        s_out = sem("stored")

        def ffn_pieces(f):
            rest, main = WA_FFN - WA[f], WA[f]
            ps = [("x0", "a", 0, main + c, c, 10) for c in range(0, rest, 512)]
            ps += [("a9", "a", 1, c, c, 9) for c in range(0, main, 512)]
            ps += [("x1", "a", 1, main + c, c, 11) for c in range(0, rest, 512)]
            ps += [(f"b{s}", "b", s, c, c, 8 + s) for s in range(2) for c in (0, 512)]
            return ps

        pieces = [ffn_pieces(f) for f in range(2)]

        def pieces_until(f, last):
            return max(i + 1 for i, p in enumerate(pieces[f]) if p[0] == last)

        def ln_dve_stats(dve, st, t):
            i = 8 * st + t
            nc.vector.bn_stats(ln_stats[:, t % 2, :], x[:, t, :]).then_inc(ln["stats"], 1)
            dve.wait_ge(ln["stats"], i + 1)
            nc.vector.bn_aggr(ln_mv[:, t, :], ln_stats[:, t % 2, :]).then_inc(ln["mv"], 1)
            dve.wait_ge(ln["mv"], i + 1)
            nc.vector.tensor_scalar(ln_ve[:, t:t + 1], ln_mv[:, t, 1:2], LN_EPS, None, ALU.add).then_inc(ln["ve"], 1)

        def ln_pool(pool, st, t):
            i = 8 * st + t
            pool.wait_ge(ln["ve"], i + 1)
            nc.gpsimd.tensor_tensor(ln_r[:, t:t + 1], ln_ve[:, t:t + 1], neg_half[:, 0:1], ALU.pow).then_inc(ln["r"], 1)

        def ln_dve_scale(dve, st, t):
            i = 8 * st + t
            dve.wait_ge(ln["r"], i + 1)
            if i >= 4:
                dve.wait_ge(ln["turned"], i - 3)
            nc.vector.tensor_scalar(xn[:, t % 4, :], x[:, t, :], ln_mv[:, t, 0:1], ln_r[:, t:t + 1],
                                    ALU.subtract, ALU.mult).then_inc(ln["xn"], 1)

        def ln_pe(pe, st, t, bk):
            i = 8 * st + t
            pe.wait_ge(ln["xn"], i + 1)
            for c in range(NC):
                mm = pe.transpose(bank[bk][:, c * P:(c + 1) * P], xn[:, t % 4, c * P:(c + 1) * P], ident)
            mm.then_inc(ln["turned"], 1)

        def ln_act(act, st, t, bk):
            i = 8 * st + t
            act.wait_ge(ln["turned"], i + 1)
            src = bank[bk][:, 0:D].rearrange("p (c t) -> p c t", c=NC)
            nc.scalar.copy(xT[0][:, :, t * P:(t + 1) * P], src).then_inc(ln["hi"], 1)

        def ln_dve_lo(dve, st, t, bk):
            i = 8 * st + t
            dve.wait_ge(ln["hi"], i + 1)
            src = bank[bk][:, 0:D].rearrange("p (c t) -> p c t", c=NC)
            nc.vector.tensor_tensor(xT[1][:, :, t * P:(t + 1) * P], src, xT[0][:, :, t * P:(t + 1) * P].bitcast(F32),
                                    ALU.subtract).then_inc(ln["lo"], 1)

        def pe_scores(pe, L, it, c):
            s = at[L]
            if live(it, c):
                u = c % 8
                b, hh = u // 2, u % 2
                need(pe, s["max"], it, 2 * c - 2, 2)
                if L == 0:
                    need(pe, s["tqev"], it, c - hh + 2)
                    q, k = hh, 2
                else:
                    need(pe, s["qkev"], it, c - u + 4 * (b // 2) + 2 * hh + 2)
                    q, k = 2 * hh, 2 * hh + 1
                ps = bank[S_BANK + c % 2]
                t0 = b * D
                pe.matmul(ps[:, 0:128], qk[:, q, t0:t0 + 128], qk[:, k, t0:t0 + 128], start=True, stop=True)
                pe.matmul(ps[:, 128:384], qk[:, q, t0 + 128:t0 + 256], qk[:, k, t0:t0 + 256],
                          start=True, stop=True).then_inc(s["scores"], 1)

        def pe_slot(pe, L, it, c):
            s = at[L]
            pe_scores(pe, L, it, c if c < TAIL_SLOT else c + 1)
            m = c - 6
            if live(it, m):
                t, slot = m % 8, (m // 8) % 2
                need(pe, s["elo"], it, m - t % 2 + 2)
                if t == 0:
                    need_pairs(pe, s["b"], it, 4 * (m // 8 + 1), 4)
                need(pe, s["opadd"], it, m)
                for i, (h, (l, r)) in enumerate([(h, p) for h in range(2) for p in PASSES]):
                    mm = pe.matmul(bank[OP_BANK][:, 0:D], enc[l][:, h, t * P:(t + 1) * P],
                                   b_w[slot][r][:, h * D:(h + 1) * D], start=i == 0, stop=i == 5)
                mm.then_inc(s["op"], 1)
            m = c + 5
            if live(it, m):
                t, slot = m % 8, (m // 8) % 2
                if t == 0:
                    if it is None and m == 0:
                        pe.wait_ge(s["a0"], 1 if L == 0 else 4)
                    else:
                        need_pairs(pe, s["a"], it, 4 * (m // 8), 4)
                if it is None and m < 8:
                    ready = m + 1 if L == 0 else 4 * (m // 4 + 1)
                    pe.wait_ge(ln["lo"], 16 * L + ready)
                ps = bank[PJ_BANK + m % 2]
                if L == 0:
                    need(pe, s["rot"], it, m - 1)
                    for i, (g, (l, r)) in enumerate([(g, p) for g in range(NC) for p in PASSES]):
                        mm = pe.matmul(ps[:, :], xT[l][:, g, t * P:(t + 1) * P], a_w[slot][r][:, g * 512:(g + 1) * 512],
                                       start=i == 0, stop=i == 5)
                else:
                    half, w = t // 4, t % 4
                    need(pe, s["qkev"], it, m - 1)
                    for i, (g, (l, r)) in enumerate([(g, p) for g in range(NC) for p in PASSES]):
                        mm = pe.matmul(ps[:, :], a_w[slot][l][:, g * 768 + w * P:g * 768 + (w + 1) * P],
                                       xT[r][:, g, half * 512:(half + 1) * 512], start=i == 0, stop=i == 5)
                mm.then_inc(s["proj"], 1)
            if L == 1:
                m = c + 5
                if live(it, m):
                    t, slot = m % 8, (m // 8) % 2
                    if it is None and m < 8:
                        pe.wait_ge(ln["lo"], 16 + 4 * (m // 4 + 1))
                    need(pe, s["vev"], it, m)
                    for i, (g, (l, r)) in enumerate([(g, p) for g in range(NC) for p in PASSES]):
                        mm = pe.matmul(bank[TQ_BANK][:, 0:D], xT[l][:, g, t * P:(t + 1) * P],
                                       a_w[slot][r][:, g * 768 + 512:(g + 1) * 768], start=i == 0, stop=i == 5)
                    mm.then_inc(s["vproj"], 1)
            m = c - 2
            if live(it, m):
                need(pe, s["pnorm"], it, 2 * m + 2, 2)
                need(pe, s["ptev"], it, m)
                for j in range(3):
                    mm = pe.transpose(bank[PT_BANK][:, j * P:(j + 1) * P], probs[:, m % 4, j * P:(j + 1) * P], ident)
                mm.then_inc(s["pt"], 1)
            m = c - 3
            if live(it, m):
                u = m % 8
                b, hh = u // 2, u % 2
                vc = 0 if L == 0 else hh * DH
                need(pe, s["ptev"], it, m + 1)
                need(pe, s["vev"], it, m - hh + 2)
                need(pe, s["elo"], it, m)
                pe.matmul(bank[O_BANK][:, 0:256], v[:, m // 8 % 2, 2 * b, vc:vc + DH], probs_t[:, m % 2, 0:256],
                          start=True, stop=False, skip_group_check=True)
                pe.matmul(bank[O_BANK][:, 128:256], v[:, m // 8 % 2, 2 * b + 1, vc:vc + DH], probs_t[:, m % 2, 256:384],
                          start=False, stop=True, skip_group_check=True).then_inc(s["pv"], 1)
            if L == 0:
                m = c + 3
                if live(it, m):
                    need(pe, s["roped"], it, m + 1)
                    need(pe, s["tqev"], it, m)
                    for j in range(3):
                        mm = pe.transpose(bank[TQ_BANK][:, j * P:(j + 1) * P], rot_a[:, m % 2, j * P:(j + 1) * P], ident)
                    mm.then_inc(s["tq"], 1)
            if c == TAIL_SLOT - 1:
                pe_scores(pe, L, it, TAIL_SLOT)

        def act_slot(act, L, it, c):
            s = at[L]
            m = c - 3
            if live(it, m):
                need(act, s["pt"], it, m + 1)
                need(act, s["pv"], it, m - 1)
                nc.scalar.copy(probs_t[:, m % 2, :], bank[PT_BANK][:, 0:384]).then_inc(s["ptev"], 1)
            m = c - 4
            if live(it, m):
                u = m % 8
                b, hh = u // 2, u % 2
                need(act, s["pv"], it, m + 1)
                need(act, s["op"], it, m - hh - 6)
                nc.scalar.copy(enc[0][:, hh, b * D:(b + 1) * D], bank[O_BANK][:, 0:D]).then_inc(s["ehi"], 1)
            m = c + 4
            if live(it, m):
                t = m % 8
                need(act, s["proj"], it, m + 1)
                if L == 0:
                    need(act, s["ss"], it, m)
                    nc.scalar.activation(squares[:, :], bank[PJ_BANK + m % 2][:, 0:384], ACT.Square).then_inc(s["sq"], 1)
                    need(act, s["pv"], it, m - t % 2 - 14)
                    nc.scalar.copy(v[:, m // 8 % 2, t, 0:DH], bank[PJ_BANK + m % 2][:, 384:512]).then_inc(s["vev"], 1)
                else:
                    half, w = t // 4, t % 4
                    need(act, s["scores"], it, m - t + 4 * half - 4)
                    if it is None and m in (0, 2):
                        act.wait_ge(ff[0]["lo"], 10 + m)
                        act.wait_ge(ff[0]["lo23"], 2 + m)
                    nc.scalar.copy(qk[:, w, half * 512:(half + 1) * 512], bank[PJ_BANK + m % 2][:, :]).then_inc(s["qkev"], 1)
            if L == 0:
                m = c + 2
                if live(it, m):
                    t = m % 8
                    need(act, s["tq"], it, m + 1)
                    need(act, s["scores"], it, m - t % 2 - 6)
                    nc.scalar.copy(qk[:, 0:3, t * P:(t + 1) * P],
                                   bank[TQ_BANK][:, 0:384].rearrange("p (a t) -> p a t", a=3)).then_inc(s["tqev"], 1)
            if live(it, c):
                u = c % 8
                b, hh = u // 2, u % 2
                need(act, s["nb"], it, c + 1)
                need(act, s["pt"], it, c - 3)
                for r, (c0, c1) in enumerate(((0, 128), (128, 384))):
                    scale = rms_r[:, 2 * b + r, hh:hh + 1] if L == 0 else float(DH) ** -0.5
                    nc.scalar.activation(probs[:, c % 4, c0:c1], scores[:, c % 2, c0:c1], ACT.Exp,
                                         bias=negmax[:, c % 2, r:r + 1], scale=scale,
                                         accum_out=rowsum[:, c % 4, r:r + 1]).then_inc(s["exp"], 1)

        def dve_normalise(dve, L, it, c):
            s, m = at[L], c - 1
            if live(it, m):
                need(dve, s["exp"], it, 2 * m + 2, 2)
                nc.vector.reciprocal(rinv[:, m % 4, :], rowsum[:, m % 4, :]).then_inc(s["rinv"], 1)
                need(dve, s["rinv"], it, m + 1)
                for r, (c0, c1) in enumerate(((0, 128), (128, 384))):
                    nc.vector.tensor_scalar(probs[:, m % 4, c0:c1], probs[:, m % 4, c0:c1], rinv[:, m % 4, r:r + 1], None,
                                            ALU.mult).then_inc(s["pnorm"], 1)

        def dve_residual(dve, L, it, c):
            s, m = at[L], c - 7
            if live(it, m):
                need(dve, s["op"], it, m + 1)
                nc.vector.tensor_tensor(x[:, m % 8, :], bank[OP_BANK][:, 0:D], x[:, m % 8, :], ALU.add).then_inc(s["opadd"], 1)

        def dve_enc_lo(dve, L, it, c):
            s, m = at[L], c - 4
            if live(it, m):
                w = m % 8
                need(dve, s["ehi"], it, m + 1)
                dst = slice((w // 2) * D, (w // 2 + 1) * D)
                nc.vector.tensor_tensor(enc[1][:, w % 2, dst], bank[O_BANK][:, 0:D], enc[0][:, w % 2, dst].bitcast(F32),
                                        ALU.subtract).then_inc(s["elo"], 1)

        def dve_scores_wait(dve, L, it, c):
            s = at[L]
            if live(it, c):
                need(dve, s["scores"], it, c + 1)
                need(dve, s["exp"], it, 2 * c - 2, 2)

        def dve_maxima(dve, L, it, c):
            s = at[L]
            if live(it, c):
                b, hh = c % 8 // 2, c % 2
                for r, (c0, c1) in enumerate(((0, 128), (128, 384))):
                    nc.vector.tensor_tensor_reduce(out=scores[:, c % 2, c0:c1], in0=bank[S_BANK + c % 2][:, c0:c1],
                                                   in1=mask[L][:, c0:c1], scale=1.0, scalar=LOW, op0=ALU.add, op1=ALU.max,
                                                   accum_out=rowmax[:, c % 2, r:r + 1]).then_inc(s["max"], 1)
                need(dve, s["max"], it, 2 * c + 2, 2)
                if L == 0:
                    need(dve, s["rp"], it, c - hh + 2)
                    nc.vector.scalar_tensor_tensor(out=negmax[:, c % 2, :], in0=rowmax[:, c % 2, :], scalar=-1.0,
                                                   in1=rms_r[:, 2 * b:2 * b + 2, hh], op0=ALU.mult,
                                                   op1=ALU.mult).then_inc(s["nb"], 1)
                else:
                    nc.vector.tensor_scalar(negmax[:, c % 2, :], rowmax[:, c % 2, :], -float(DH) ** -0.5, None,
                                            ALU.mult).then_inc(s["nb"], 1)

        def dve_slot(dve, L, it, c):
            s = at[L]
            if c < TAIL_SLOT:
                dve_normalise(dve, L, it, c)
                dve_residual(dve, L, it, c)
                dve_scores_wait(dve, L, it, c)
                dve_enc_lo(dve, L, it, c)
                dve_maxima(dve, L, it, c)
            else:
                dve_scores_wait(dve, L, it, c)
                dve_maxima(dve, L, it, c)
                dve_normalise(dve, L, it, c)
                dve_residual(dve, L, it, c)
                dve_enc_lo(dve, L, it, c)
            m = c + 4
            if live(it, m):
                t = m % 8
                if L == 0:
                    ps = bank[PJ_BANK + m % 2]
                    need(dve, s["sq"], it, m + 1)
                    nc.vector.reduce_sum(sumsq[:, m % 2, :], squares[:, :].rearrange("p (a d) -> p a d", a=3),
                                         AX_X).then_inc(s["ss"], 1)
                    need(dve, s["vev"], it, m + 1)
                    need(dve, s["tq"], it, m - 1)
                    nc.vector.tensor_tensor(rot_a[:, m % 2, :], ps[:, 0:384],
                                            cos_t[:, t % 2, :, :].rearrange("p a d -> p (a d)"), ALU.mult)
                    need(dve, s["ss"], it, m + 1)
                    need(dve, s["rp"], it, m - 1)
                    nc.vector.tensor_scalar(meansq[:, m % 2, :], sumsq[:, m % 2, :], 1.0 / DH, RMS_EPS,
                                            ALU.mult, ALU.add).then_inc(s["ms"], 1)
                    need(dve, s["radd"], it, m - 1)
                    nc.vector.tensor_tensor(
                        rot_b[:, m % 2, :].rearrange("p (a h d) -> p a h d", a=3, h=2),
                        ps[:, 0:384].rearrange("p (a h d) -> p a h d", a=3, h=2)[:, :, ::-1, :],
                        sin_t[:, t % 2, :, :].rearrange("p a (h d) -> p a h d", h=2), ALU.mult).then_inc(s["rot"], 1)
                else:
                    need(dve, s["vproj"], it, m + 1)
                    need(dve, s["pv"], it, m - t % 2 - 14)
                    nc.vector.tensor_copy(v[:, m // 8 % 2, t, :], bank[TQ_BANK][:, 0:D]).then_inc(s["vev"], 1)

        def split(hi, lo, src, eng, s_hi, wait, s_lo):
            nc.gpsimd.tensor_tensor(hi, src, zero[:, 0:1].broadcast_to(list(src.shape)), ALU.add).then_inc(s_hi, 1)
            wait()
            nc.gpsimd.tensor_tensor(lo, src, hi.bitcast(F32), ALU.subtract).then_inc(s_lo, 1)

        def pool_slot(pool, L, it, c):
            s = at[L]
            if L == 0:
                m = c + 3
                if live(it, m):
                    t = m % 8
                    need(pool, s["ms"], it, m + 1)
                    need(pool, s["exp"], it, 2 * (m - t % 2) - 12, 2)
                    nc.gpsimd.tensor_tensor(rms_r[:, t, :], meansq[:, m % 2, :], neg_half[:, 0:3], ALU.pow).then_inc(s["rp"], 1)
                    need(pool, s["rot"], it, m + 1)
                    nc.gpsimd.tensor_tensor(rot_a[:, m % 2, :], rot_a[:, m % 2, :], rot_b[:, m % 2, :],
                                            ALU.add).then_inc(s["radd"], 1)
                    need(pool, s["radd"], it, m + 1)
                    need(pool, s["rp"], it, m + 1)
                    nc.gpsimd.tensor_tensor(rot_a[:, m % 2, 256:384], rot_a[:, m % 2, 256:384],
                                            rms_r[:, t, 2:3].broadcast_to([P, DH]), ALU.mult).then_inc(s["roped"], 1)
            m = c + 5
            if (it is not None or 0 <= m < 64) and m % 2 == 0:
                pair, part = m // 8 + 1, m % 8 // 2
                w, slot = WA[L] // 4, pair % 2
                if part == 0:
                    need_pairs(pool, raw_as[L][slot], it, 16 * (pair // 2 + 1), 8)
                    need(pool, s["proj"], it, 8 * (pair - 1))
                    if L == 1:
                        need(pool, s["vproj"], it, 8 * (pair - 1))
                    if L == 1 and it is None and pair == 1:
                        pool.wait_ge(ff[0]["up"], 16)
                cs = slice(part * w, (part + 1) * w)
                done = 4 * (pair - 1) + part + 1
                split(a_w[slot][0][:, cs], a_w[slot][1][:, cs], raw_a[:, slot, cs], pool, s["ahi"],
                      lambda: need_pairs(pool, s["ahi"], it, done, 4), s["a"])
            m = c - 6
            if (it is not None or -8 <= m < 56) and m % 2 == 0:
                pair, part = m // 8 + 1, m % 8 // 2
                w, slot = WB // 4, pair % 2
                if part == 0:
                    need_pairs(pool, raw_bs[L][slot], it, 16 * (pair // 2 + 1), 8)
                    need(pool, s["op"], it, 8 * (pair - 1))
                    if L == 1 and it is None and pair == 0:
                        pool.wait_ge(ff[0]["down"], 12)
                    if L == 1 and it is None and pair == 1:
                        pool.wait_ge(ff[0]["down"], 16)
                cs = slice(part * w, (part + 1) * w)
                done = 4 * pair + part + 1
                split(b_w[slot][0][:, cs], b_w[slot][1][:, cs], raw_b[:, slot, cs], pool, s["bhi"],
                      lambda: need_pairs(pool, s["bhi"], it, done, 4), s["b"])

        def slots(eng, L, body, head, tail):
            for c in range(FIRST_SLOT, LOOP_FROM):
                body(eng, L, None, c)
                head(c)
            with eng.Fori(0, LOOPS) as it:
                for j in range(LOOP_STEP):
                    body(eng, L, it, LOOP_FROM + j)
            for c in range(LOOP_FROM + LOOP_STEP * LOOPS, LAST_SLOT + 1):
                body(eng, L, None, c)
                tail(c - FIRST_TAIL)

        def pe_gate_up(pe, f, k, tiles=range(4)):
            s, L = ff[f], at[f]
            th, t = k // 2, k % 2
            base = 16 * f + 8
            for j in tiles:
                i = 4 * k + j
                r = i % 3
                if j == 0:
                    pe.wait_ge(ln["lo"], base + 4 * (th + 1))
                    if k < 2:
                        if k == 0:
                            pe.wait_ge(L["a"], 32)
                        pe.wait_ge(s["w"], pieces_until(f, "x0" if t == 0 else "x1"))
                if i >= 3:
                    pe.wait_ge(s["silu"], i - 2)
                    pe.wait_ge(s["h"], i - 2)
                elif i == 0:
                    pe.wait_ge(L["max"], 2 * UNITS)
                    if f == 1:
                        pe.wait_ge(s_hadev, 4)
                elif i == 1:
                    pe.wait_ge(L["rot" if f == 0 else "qkev"], UNITS)
                else:
                    pe.wait_ge(L["ptev"], UNITS)
                    pe.wait_ge(ln["lo"], base + 4)
                for up in range(2):
                    ps = bank[2 * r + up]
                    for q, (g, (l, rr)) in enumerate([(g, p) for g in range(NC) for p in PASSES]):
                        c0 = g * HID + up * 512 + j * P
                        mm = pe.matmul(ps[:, :], a_w[t][l][:, c0:c0 + P], xT[rr][:, g, th * 512:(th + 1) * 512],
                                       start=q == 0, stop=q == 5)
                    mm.then_inc(s["up" if up else "gate"], 1)
                if k == 0:
                    for tile in ((4,), (5, 6), (7,), ())[j]:
                        if tile == 4:
                            pe.wait_ge(L["elo"], UNITS)
                        elif tile == 5:
                            pe.wait_ge(L["opadd"], UNITS)
                        else:
                            pe.wait_ge(ln["lo"], base + tile - 1)
                        ln_pe(pe, 2 * f + 1, tile, 6 + tile % 2)

        def pe_down(pe, f, k, tiles=range(4)):
            s, L = ff[f], at[f]
            t = k % 2
            for tt in tiles:
                d = 4 * k + tt
                if tt == 0:
                    pe.wait_ge(s["hi"], 4 * k + 4)
                    if f == 0 and k >= 2:
                        pe.wait_ge(s["lo"], 2 * k + 6)
                        pe.wait_ge(s["lo23"], 2 * k - 2)
                    else:
                        pe.wait_ge(s["lo"], 4 * k + 4)
                    if k < 2:
                        pe.wait_ge(s["w"], pieces_until(f, f"b{t}"))
                if d < 2:
                    pe.wait_ge(ln["lo"], 16 * f + 16)
                if d >= 2:
                    pe.wait_ge(s["xadd"], d - 1)
                for q, (j, (l, r)) in enumerate([(j, p) for j in range(4) for p in PASSES]):
                    mm = pe.matmul(bank[6 + d % 2][:, 0:D], encf[l][:, j, tt * P:(tt + 1) * P],
                                   b_w[t][r][:, j * D:(j + 1) * D], start=q == 0, stop=q == 11)
                mm.then_inc(s["down"], 1)

        def pe_hadamard(pe, q):
            pe.wait_ge(at[1]["max"], 2 * UNITS)
            pe.wait_ge(s_w2lo, q + 1)
            if q >= 2:
                pe.wait_ge(s_hadev, q - 1)
            for r in range(2):
                mm = pe.matmul(bank[S_BANK + q % 2][:, :], had_r[:, :], w2_s[r][:, :], start=r == 0, stop=r == 1)
            mm.then_inc(s_hadmm, 1)

        def pe_ffn0(pe):
            pe_gate_up(pe, 0, 0)
            pe_gate_up(pe, 0, 1)
            pe_gate_up(pe, 0, 2, (0, 1, 2))
            pe_down(pe, 0, 0)
            pe_gate_up(pe, 0, 2, (3,))
            pe_gate_up(pe, 0, 3, (0, 1))
            pe_down(pe, 0, 1)
            pe_gate_up(pe, 0, 3, (2, 3))
            for t in range(4):
                pe.wait_ge(ff[0]["h"], 14 + t // 2)
                ln_pe(pe, 2, t, 2 + t)
            pe_down(pe, 0, 2)

        def pe_ffn1(pe):
            pe_gate_up(pe, 1, 0)
            pe_gate_up(pe, 1, 1)
            pe_down(pe, 1, 0)
            pe_gate_up(pe, 1, 2)
            pe_down(pe, 1, 1)
            pe_gate_up(pe, 1, 3)
            pe_down(pe, 1, 2)
            pe_down(pe, 1, 3)

        def act_silu(act, f, i):
            s = ff[f]
            act.wait_ge(s["gate"], i + 1)
            if i >= 2:
                act.wait_ge(s["h"], i - 1)
            nc.scalar.activation(gate[:, i % 2, :], bank[2 * (i % 3)][:, :], ACT.Silu).then_inc(s["silu"], 1)

        def act_ln_gate(act, f):
            st = 2 * f + 1
            ln_act(act, st, 4, 6)
            act_silu(act, f, 0)
            ln_act(act, st, 5, 7)
            ln_act(act, st, 6, 6)
            act_silu(act, f, 1)
            ln_act(act, st, 7, 7)
            act_silu(act, f, 2)
            act_silu(act, f, 3)

        def act_hi(act, f, k):
            s = ff[f]
            if k == 0:
                act.wait_ge(at[f]["op"], UNITS)
            else:
                act.wait_ge(s["down"], 4 * k)
            for j in range(4):
                act.wait_ge(s["hs" if f == 0 else "h"], 4 * k + j + 1)
                nc.scalar.copy(encf[0][:, j, :], hid[:, k % 2, j, :]).then_inc(s["hi"], 1)

        def act_hadamard(act, q):
            act.wait_ge(s_hadmm, q + 1)
            nc.scalar.mul(w2_a[:, 2 * q:2 * q + 2, :].rearrange("p a d -> p (a d)"), bank[S_BANK + q % 2][:, :],
                          float(HID) ** -0.5).then_inc(s_hadev, 1)

        def act_abs(act, i):
            k, j = i // 4, i % 4
            act.wait_ge(ff[0]["h"], i + 1)
            if i == 0:
                act.wait_ge(at[0]["pv"], UNITS)
            elif k and j == 0:
                act.wait_ge(ff[0]["cmp"], 6 * k)
            nc.scalar.activation(mag[:, j, :], hid[:, k % 2, j, :], ACT.Abs).then_inc(ff[0]["abs"], 1)

        def act_ffn0(act):
            act_ln_gate(act, 0)
            for i in range(4):
                act_abs(act, i)
            for k in range(3):
                i = 4 * (k + 1)
                act_silu(act, 0, i)
                act_silu(act, 0, i + 1)
                act_silu(act, 0, i + 2)
                act_abs(act, i)
                act_abs(act, i + 1)
                act_silu(act, 0, i + 3)
                act_abs(act, i + 2)
                act_hi(act, 0, k)
                act_abs(act, i + 3)
            for t in range(4):
                ln_act(act, 2, t, 2 + t)

        def act_ffn1(act):
            act_ln_gate(act, 1)
            for k in range(4):
                if k:
                    act_silu(act, 1, 4 * k + 2)
                    act_silu(act, 1, 4 * k + 3)
                if k < 3:
                    act_silu(act, 1, 4 * k + 4)
                    act_silu(act, 1, 4 * k + 5)
                act_hi(act, 1, k)

        def dve_hidden(dve, f, i):
            s = ff[f]
            k, j = i // 4, i % 4
            dve.wait_ge(s["silu"], i + 1)
            dve.wait_ge(s["up"], i + 1)
            if i == 0:
                dve.wait_ge(at[f]["scores"], UNITS)
            if k >= 2:
                dve.wait_ge(s["hi"], 4 * k - 8 + j + 1)
                dve.wait_ge(s["lo"], 4 * k - 8 + j + 1)
            nc.vector.tensor_tensor(hid[:, k % 2, j, :], bank[2 * (i % 3) + 1][:, :], gate[:, i % 2, :],
                                    ALU.mult).then_inc(s["h"], 1)

        def dve_ln_hidden(dve, f):
            st = 2 * f + 1
            ln_dve_scale(dve, st, 7)
            ln_dve_lo(dve, st, 4, 6)
            dve_hidden(dve, f, 0)
            ln_dve_lo(dve, st, 5, 7)
            ln_dve_lo(dve, st, 6, 6)
            dve_hidden(dve, f, 1)
            ln_dve_lo(dve, st, 7, 7)
            dve_hidden(dve, f, 2)
            dve_hidden(dve, f, 3)

        def dve_xadd(dve, f, k, tt):
            s = ff[f]
            d, t = 4 * k + tt, 4 * (k // 2) + tt
            dve.wait_ge(s["down"], d + 1)
            nc.vector.tensor_tensor(x[:, t, :], bank[6 + d % 2][:, 0:D], x[:, t, :], ALU.add).then_inc(s["xadd"], 1)
            if f == 0 and k % 2 == 1:
                dve.wait_ge(s["xadd"], d + 1)
                ln_dve_stats(dve, 2, t)

        def dve_compare(dve, k, n):
            s = ff[0]
            a, b = ((0, 1), (0, 2), (1, 2), (0, 3), (1, 3), (2, 3))[n]
            dve.wait_ge(s["abs"], 4 * k + b + 1)
            nc.vector.tensor_tensor(cmp[:, n, :], mag[:, a, :], mag[:, b, :], ALU.is_ge).then_inc(s["cmp"], 1)

        s_cnt = sem("kept_counts")

        C01, C02, C12, C03, C13, C23 = range(6)
        KEEP = ((C01, C02, C03, ALU.add, ALU.is_ge, 1.5), (C12, C13, C01, ALU.subtract, ALU.is_ge, 0.5),
                (C02, C12, C23, ALU.subtract, ALU.is_lt, 0.5), (C03, C13, C23, ALU.add, ALU.is_lt, 1.5))

        def dve_count(dve, k, step):
            for j, (a, b, c, op, _, _) in enumerate(KEEP):
                if step == 0:
                    if j == 0:
                        dve.wait_ge(ff[0]["cmp"], 6 * k + 6)
                    nc.vector.tensor_tensor(cnt[:, j, :], cmp[:, a, :], cmp[:, b, :], ALU.add).then_inc(s_cnt, 1)
                else:
                    dve.wait_ge(s_cnt, 8 * k + j + 1)
                    nc.vector.tensor_tensor(cnt[:, j, :], cnt[:, j, :], cmp[:, c, :], op).then_inc(s_cnt, 1)

        def dve_keep(dve, k, tiles=range(4)):
            for j in tiles:
                keep, than = KEEP[j][4:]
                dve.wait_ge(s_cnt, 8 * k + 4 + j + 1)
                h = hid[:, k % 2, j, :]
                nc.vector.scalar_tensor_tensor(out=h, in0=cnt[:, j, :], scalar=than, in1=h, op0=keep,
                                               op1=ALU.mult).then_inc(ff[0]["hs"], 1)

        def dve_lo23(dve, k):
            for j in (2, 3):
                dve.wait_ge(ff[0]["hi"], 4 * k + j + 1)
                nc.vector.tensor_tensor(encf[1][:, j, :], hid[:, k % 2, j, :], encf[0][:, j, :].bitcast(F32),
                                        ALU.subtract).then_inc(ff[0]["lo23"], 1)

        def dve_ffn0(dve):
            dve_ln_hidden(dve, 0)
            for k in range(3):
                i = 4 * (k + 1)
                for n in range(4):
                    dve_compare(dve, k, n)
                dve_hidden(dve, 0, i)
                for n in range(4, 6):
                    dve_compare(dve, k, n)
                dve_count(dve, k, 0)
                dve_hidden(dve, 0, i + 1)
                dve_count(dve, k, 1)
                if k == 2:
                    for tt in range(4):
                        dve_xadd(dve, 0, 1, tt)
                        dve_keep(dve, 2, (tt,))
                dve_hidden(dve, 0, i + 2)
                if k == 1:
                    for tt in range(4):
                        dve_xadd(dve, 0, 0, tt)
                if k < 2:
                    dve_keep(dve, k)
                else:
                    for t in range(4):
                        ln_dve_scale(dve, 2, t)
                    dve_lo23(dve, 2)
                dve_hidden(dve, 0, i + 3)
            for t in range(4):
                ln_dve_lo(dve, 2, t, 2 + t)
            for n in range(6):
                dve_compare(dve, 3, n)
                if 1 <= n <= 4:
                    dve_xadd(dve, 0, 2, n - 1)
            dve_count(dve, 3, 0)

        def dve_ffn1(dve):
            s = ff[1]
            dve_ln_hidden(dve, 1)
            for k in range(4):
                if k:
                    dve_hidden(dve, 1, 4 * k + 2)
                    dve_hidden(dve, 1, 4 * k + 3)
                    for tt in range(4):
                        dve_xadd(dve, 1, k - 1, tt)
                if k < 3:
                    dve_hidden(dve, 1, 4 * k + 4)
                    dve_hidden(dve, 1, 4 * k + 5)
                for j in range(4):
                    dve.wait_ge(s["hi"], 4 * k + j + 1)
                    nc.vector.tensor_tensor(encf[1][:, j, :], hid[:, k % 2, j, :], encf[0][:, j, :].bitcast(F32),
                                            ALU.subtract).then_inc(s["lo"], 1)
            for tt in range(4):
                dve_xadd(dve, 1, 3, tt)

        def pool_piece(pool, f, n):
            what, ring, slot, col, src, load = pieces[f][n]
            s, L = ff[f], at[f]
            if ring == "a":
                pool.wait_ge(raw_as[f][slot], 16 * (load // 2 + 1))
                if what == "a9":
                    pool.wait_ge(L["proj"], UNITS)
                    if f == 1:
                        pool.wait_ge(L["vproj"], UNITS)
                source, dst = raw_a[:, slot, src:src + 512], a_w[slot]
            else:
                pool.wait_ge(L["op"], UNITS - 8 * (1 - slot))
                if f == 0:
                    pool.wait_ge(raw_bs[0][slot], 16 * (load // 2 + 1))
                    source = raw_b[:, slot, src:src + 512]
                else:
                    pool.wait_ge(s_hadev, 4)
                    a = 4 * slot + src // D
                    source = w2_a[:, a:a + 2, :].rearrange("p a d -> p (a d)")
                dst = b_w[slot]
            split(dst[0][:, col:col + 512], dst[1][:, col:col + 512], source, pool, s["whi"],
                  lambda: pool.wait_ge(s["whi"], n + 1), s["w"])

        def pool_tail(pool, f):
            def tail(t):
                n = t + FIRST_TAIL - (LOOP_FROM + LOOP_STEP * LOOPS)
                if n < 4:
                    pool_piece(pool, f, n)
                if t >= 0:
                    ln_pool(pool, 2 * f + 1, t)
                if f == 1 and 1 <= t <= 3:
                    w2_part(pool, t)
            return tail

        def w2_part(pool, q):
            if q:
                pool.wait_ge(s_hadmm, q)
            split(w2_s[0][:, :], w2_s[1][:, :], w2_b[:, 2 * q:2 * q + 2, :].rearrange("p a d -> p (a d)"), pool, s_w2hi,
                  lambda: pool.wait_ge(s_w2hi, q + 1), s_w2lo)

        def pool_head(c):
            if c == -3:
                for t in range(4, 8):
                    ln_pool(nc.gpsimd, 2, t)
            if c == 1:
                nc.gpsimd.wait_ge(s_w2, 16)
                nc.gpsimd.wait_ge(ff[0]["hs"], 16)
            if 1 <= c <= 6:
                n = c - 1
                src, dst = ((w2_a, w2_b), (w2_b, w2_a))[n // 2 % 2]
                h = 4 >> n // 2
                a = src[:, :, :].rearrange("p (g s h) d -> p g s (h d)", s=2, h=h)
                b = dst[:, :, :].rearrange("p (g s h) d -> p g s (h d)", s=2, h=h)
                if n >= 2:
                    nc.gpsimd.wait_ge(s_bf, 2 * (n // 2))
                nc.gpsimd.tensor_tensor(b[:, :, n % 2, :], a[:, :, 0, :], a[:, :, 1, :],
                                        (ALU.add, ALU.subtract)[n % 2]).then_inc(s_bf, 1)
            if c == 7:
                nc.gpsimd.wait_ge(s_bf, 6)
                w2_part(nc.gpsimd, 0)

        def pool_lo(pool, k):
            s = ff[0]
            for j in range(4 if k < 2 else 2):
                pool.wait_ge(s["hi"], 4 * k + j + 1)
                pool.wait_ge(s["down"], 4 * k) if k else pool.wait_ge(at[0]["op"], UNITS)
                nc.gpsimd.tensor_tensor(encf[1][:, j, :], hid[:, k % 2, j, :], encf[0][:, j, :].bitcast(F32),
                                        ALU.subtract).then_inc(s["lo"], 1)

        block = ctx.enter_context(nc.Block())

        @block.sync
        def _(sp):
            x_v = x_in.rearrange("(t p) d -> p t d", p=P)
            for i in range(4):
                sp.dma_start(x[:, 2 * i:2 * i + 2, :], x_v[:, 2 * i:2 * i + 2, :]).then_inc(s_x[i], 16)
            for L in range(2):
                s = at[L]

                def load(it, pair):
                    slot = pair % 2
                    if L == 1 and it is None and pair < 2:
                        sp.wait_ge(ff[0]["w"], pieces_until(0, f"x{pair}"))
                        sp.wait_ge(ff[0]["w"], pieces_until(0, f"b{pair}"))
                    if it is None and pair == 2:
                        sp.wait_ge(s["a0"], 1 if L == 0 else 4)
                    else:
                        need_pairs(sp, s["a"], it, 4 * (pair - 2), 4)
                    n = pair if it is None else it * 2 + pair
                    if not (L == 0 and it is None and pair == 0):
                        sp.dma_start(raw_a[:, slot, 0:WA[L]], wa[L][n]).then_inc(raw_as[L][slot], 16)
                    if it is not None or pair < PAIRS:
                        need_pairs(sp, s["b"], it, 4 * (pair - 1), 4)
                        sp.dma_start(raw_b[:, slot, 0:WB], wb[L][n]).then_inc(raw_bs[L][slot], 16)

                for pair in range(4):
                    load(None, pair)
                with sp.Fori(0, 2) as it:
                    load(it, 4)
                    load(it, 5)
                if L == 0:
                    sp.dma_start(w2_a[:, :, :].rearrange("p a d -> p (a d)"), w2t).then_inc(s_w2, 16)
                load(None, 8)
                load(None, 9)
                rest = WA_FFN - WA[L]
                sp.wait_ge(s["a"], 32)
                sp.dma_start(raw_a[:, 0, 0:rest], wax[L][0]).then_inc(raw_as[L][0], 16)
                if L == 0:
                    for h in range(2):
                        sp.wait_ge(s["b"], 28 + 4 * h)
                        sp.dma_start(raw_b[:, h, :], wdown0[h]).then_inc(raw_bs[0][h], 16)
                sp.wait_ge(ff[L]["w"], pieces_until(L, "a9"))
                sp.dma_start(raw_a[:, 1, 0:rest], wax[L][1]).then_inc(raw_as[L][1], 16)
            o_v = out.rearrange("(t p) d -> p t d", p=P)
            sp.wait_ge(ff[1]["xadd"], 8)
            sp.dma_start(o_v[:, 0:4, :], x[:, 0:4, :]).then_inc(s_out, 16)
            for t in range(4, 8):
                sp.wait_ge(ff[1]["xadd"], 8 + t + 1)
                sp.dma_start(o_v[:, t, :], x[:, t, :]).then_inc(s_out, 16)
            sp.wait_ge(s_out, 5 * 16)

        @block.gpsimd
        def _(pool):
            nc.gpsimd.memset(zero[:, :], 0.0).then_inc(s_zero, 1)
            nc.gpsimd.memset(neg_half[:, :], -0.5).then_inc(s_half, 1)
            pool.wait_ge(s_zero, 1)
            pool.wait_ge(s_half, 1)
            for t in range(4):
                ln_pool(pool, 0, t)
            pool.wait_ge(s_rope, 16)
            pool.wait_ge(s_scq, 1)
            for tab, c, sc in ((cos_t, cos_c, 0), (sin_t, sin_c, 2)):
                for a in range(3):
                    nc.gpsimd.tensor_tensor(tab[:, :, a, :], c, scl[:, sc + a // 2, :].unsqueeze(1).broadcast_to([P, 2, DH]),
                                            ALU.mult).then_inc(s_tab, 1)
            for t in range(4, TILES):
                ln_pool(pool, 0, t)
            slots(pool, 0, pool_slot, lambda c: None, pool_tail(pool, 0))
            for n in range(4, len(pieces[0])):
                pool_piece(pool, 0, n)
            pool.wait_ge(s_ident, 16)
            nc.gpsimd.tensor_tensor(had_r[:, :], cst[:, 128:256], zero[:, 0:1].broadcast_to([P, P]), ALU.add).then_inc(s_hadr, 1)
            pool_lo(pool, 0)
            pool_lo(pool, 1)
            pool.wait_ge(raw_as[1][0], 16)
            pool.wait_ge(ff[0]["up"], 12)
            w = WA[1] // 4
            for part in range(4):
                cs = slice(part * w, (part + 1) * w)
                split(a_w[0][0][:, cs], a_w[0][1][:, cs], raw_a[:, 0, cs], pool, at[1]["a0hi"],
                      lambda: pool.wait_ge(at[1]["a0hi"], part + 1), at[1]["a0"])
                if part == 1:
                    for t in range(4):
                        ln_pool(pool, 2, t)
                    pool_lo(pool, 2)
            pool_lo(pool, 3)
            slots(pool, 1, pool_slot, pool_head, pool_tail(pool, 1))
            for n in range(4, len(pieces[1])):
                pool_piece(pool, 1, n)

        @block.scalar
        def _(act):
            act.dma_start(cst[:, 0:256], consts[:, 0:256]).then_inc(s_ident, 16)
            act.dma_start(raw_a[:, 0, 0:WA[0]], wa[0][0]).then_inc(raw_as[0][0], 16)
            act.dma_start(scl[:, :, :], scales).then_inc(s_scl, 16)
            act.dma_start(cst[:, 256:768], consts[:, 256:768]).then_inc(s_rope, 16)
            act.dma_start(cst[:, 768:1536], consts[:, 768:1536]).then_inc(s_mask, 16)
            act.wait_ge(raw_as[0][0], 16)
            nc.scalar.copy(a_w[0][0][:, 0:WA[0]], raw_a[:, 0, 0:WA[0]]).then_inc(at[0]["a0hi"], 1)
            for t in range(4):
                ln_act(act, 0, t, 4 + t)
            for L in range(2):
                def head(c):
                    if L == 0 and c < -1:
                        ln_act(act, 0, c + 9, 6 + (c + 1) % 2)
                    elif L == 1 and c == -3:
                        act_hi(act, 0, 3)
                    elif L == 1 and c == -2:
                        for t in range(4, 8):
                            ln_act(act, 2, t, t % 2)

                def tail(t):
                    if 2 <= t < 6:
                        if t == 2:
                            act.wait_ge(at[L]["proj"], UNITS)
                            if L == 1:
                                act.wait_ge(at[L]["vproj"], UNITS)
                        ln_act(act, 2 * L + 1, t - 2, PJ_BANK + t % 2)
                    if L == 1 and 1 <= t < 5:
                        act_hadamard(act, t - 1)

                slots(act, L, act_slot, head, tail)
                (act_ffn0, act_ffn1)[L](act)

        @block.vector
        def _(dve):
            for t in range(4):
                dve.wait_ge(s_x[t // 2], 16)
                ln_dve_stats(dve, 0, t)
            for t in range(4):
                ln_dve_scale(dve, 0, t)
            dve.wait_ge(at[0]["a0hi"], 1)
            nc.vector.tensor_tensor(a_w[0][1][:, 0:WA[0]], raw_a[:, 0, 0:WA[0]], a_w[0][0][:, 0:WA[0]].bitcast(F32),
                                    ALU.subtract).then_inc(at[0]["a0"], 1)
            dve.wait_ge(s_scl, 16)
            nc.vector.tensor_scalar(scl[:, 0::2, :], scl[:, 0::2, :], ATTN_SCALE, None, ALU.mult).then_inc(s_scq, 1)
            for t in range(4):
                ln_dve_lo(dve, 0, t, 4 + t)
            for t in range(4, TILES):
                dve.wait_ge(s_x[t // 2], 16)
                ln_dve_stats(dve, 0, t)
            for t in range(4, TILES):
                ln_dve_scale(dve, 0, t)
            dve.wait_ge(s_tab, 6)
            dve.wait_ge(s_mask, 16)
            for L in range(2):
                def tail(t):
                    if 0 <= t:
                        dve.wait_ge(at[L]["opadd"], UNITS - 8 + t + 1)
                        ln_dve_stats(dve, 2 * L + 1, t)
                    if 1 <= t:
                        ln_dve_scale(dve, 2 * L + 1, t - 1)
                    if 2 <= t < 6:
                        ln_dve_lo(dve, 2 * L + 1, t - 2, PJ_BANK + t % 2)

                def head(c):
                    if L == 0 and c < -1:
                        ln_dve_lo(dve, 0, c + 9, 6 + (c + 1) % 2)
                    elif L == 1 and c == -4:
                        dve_count(dve, 3, 1)
                        dve_keep(dve, 3, (0, 1))
                    elif L == 1 and c == -3:
                        dve_keep(dve, 3, (2, 3))
                        dve_lo23(dve, 3)
                    elif L == 1 and c == -2:
                        for tt in range(4):
                            dve_xadd(dve, 0, 3, tt)
                            if tt:
                                ln_dve_scale(dve, 2, 3 + tt)
                        ln_dve_scale(dve, 2, 7)
                        for t in range(4, 8):
                            ln_dve_lo(dve, 2, t, t % 2)

                slots(dve, L, dve_slot, head, tail)
                (dve_ffn0, dve_ffn1)[L](dve)

        @block.tensor
        def _(pe):
            pe.wait_ge(s_ident, 16)
            for t in range(4):
                ln_pe(pe, 0, t, 4 + t)
            for L in range(2):
                def head(c):
                    if L == 0 and c < -1:
                        pe.wait_ge(ln["lo"], c + 8)
                        ln_pe(pe, 0, c + 9, 6 + (c + 1) % 2)
                    elif L == 1 and c == -3:
                        pe_down(pe, 0, 3)
                    elif L == 1 and c == -2:
                        pe.wait_ge(ff[0]["h"], 16)
                        for t in range(4, 8):
                            if t >= 6:
                                pe.wait_ge(ln["lo"], 16 + t - 1)
                            ln_pe(pe, 2, t, t % 2)

                def tail(t):
                    if 1 <= t < 5:
                        if t == 1:
                            pe.wait_ge(at[L]["rot" if L == 0 else "qkev"], UNITS)
                        elif t >= 3:
                            pe.wait_ge(ln["lo"], 8 * (2 * L + 1) + t - 2)
                        ln_pe(pe, 2 * L + 1, t - 1, PJ_BANK + (t - 1) % 2)
                        if L == 1:
                            pe_hadamard(pe, t - 1)

                slots(pe, L, pe_slot, head, tail)
                (pe_ffn0, pe_ffn1)[L](pe)


def shape_constants(np):
    i = np.arange(P)
    ident = np.eye(P, dtype=np.float32)
    had = np.ones((1, 1), np.float32)
    while had.shape[0] < P:
        had = np.block([[had, had], [had, -had]])
    past, window = i[None, :] <= i[:, None], i[None, :] > i[:, None]
    low = np.float32(MASKED)
    tri = np.where(past, np.float32(0), low)
    win = np.where(window, np.float32(0), low)
    mask0 = np.concatenate([tri, win, tri], 1)
    mask1 = np.concatenate([tri, np.zeros((P, P)), tri], 1)
    frac = np.arange(0, DH, 2, dtype=np.float32) / np.float32(DH)
    timescale = (np.float32(ROPE_BASE) ** frac).astype(np.float32)
    angle = np.arange(2 * P, dtype=np.float32)[:, None] / timescale
    cos, sin = np.cos(angle.astype(np.float64)), np.sin(angle.astype(np.float64))
    cos = np.concatenate([cos, cos], 1).reshape(2, P, DH).transpose(1, 0, 2).reshape(P, 2 * DH)
    sin = np.concatenate([-sin, sin], 1).reshape(2, P, DH).transpose(1, 0, 2).reshape(P, 2 * DH)
    return np.concatenate([ident, had, cos, sin, mask0, mask1], 1).astype(np.float32)


def kernel(**inputs):
    import numpy as np
    import concourse.bacc as bacc
    from concourse.bass_utils import run_bass_kernel_spmd

    a = {n: np.asarray(v) for n, v in inputs.items()}

    def rows(w):
        return w.reshape(NC, P, -1).transpose(1, 0, 2)

    q, kv = a["L0_attn_q_kernel"], a["L0_attn_kv_kernel"]
    pairs0 = [rows(np.concatenate([q[2 * p], q[2 * p + 1], kv[0, p], kv[1, p]], 1)).reshape(P, -1) for p in range(PAIRS)]
    wq, wk, wv = (a[f"L1_attn_W_{n}"].transpose(0, 2, 1) for n in "QKV")
    pairs1 = [rows(np.concatenate([wq[2 * p], wk[2 * p], wq[2 * p + 1], wk[2 * p + 1], wv[2 * p], wv[2 * p + 1]], 1))
              .reshape(P, -1) for p in range(PAIRS)]
    def by_four(w):
        return w.reshape(D, 2, P, 4).transpose(0, 1, 3, 2).reshape(D, 2, 4 * P)

    g0, u0 = by_four(a["L0_ffn_w_gate"]), by_four(a["L0_ffn_w_up"])
    g1, u1 = (a[f"L1_ffn_W{n}"].T.reshape(D, 2, 4 * P) for n in (1, 3))
    halves = [[rows(np.concatenate([g[:, t], u[:, t]], 1)).reshape(P, -1) for t in range(2)] for g, u in ((g0, u0), (g1, u1))]
    wa = [np.stack([w[:, :WA[L]] for w in (pairs0, pairs1)[L] + halves[L]]) for L in range(2)]
    wax = [np.stack([w[:, WA[L]:] for w in halves[L]]) for L in range(2)]
    wb0 = a["L0_attn_out_kernel"].reshape(PAIRS, 2, DH, D).transpose(0, 2, 1, 3).reshape(PAIRS, P, -1)
    wb1 = a["L1_attn_W_O"].T.reshape(PAIRS, 2, DH, D).transpose(0, 2, 1, 3).reshape(PAIRS, P, -1)
    down0 = a["L0_ffn_w_down"].reshape(2, P, 4 * D)
    w2t = a["L1_ffn_W2"].T.reshape(8, P, D).transpose(1, 0, 2).reshape(P, -1)
    sq, sk = a["L0_attn_q_norm_scale"], a["L0_attn_k_norm_scale"]
    swap = np.roll(np.arange(DH), DH // 2)
    scales = np.broadcast_to(np.stack([sq, sk, sq[swap], sk[swap]])[None], (P, 4, DH))
    arrays = {
        "x": a["L0_attn_x"].reshape(TOK, D), "wa0": wa[0], "wa1": wa[1], "wax0": wax[0], "wax1": wax[1],
        "wb0": wb0, "wb1": wb1, "wdown0": down0, "w2t": w2t, "consts": shape_constants(np), "scales": scales,
    }
    arrays = {n: np.ascontiguousarray(v) for n, v in arrays.items()}
    nc = bacc.Bacc("TRN2", target_bir_lowering=False, num_devices=1)
    d = {n: nc.dram_tensor(f"in_{n}", v.shape, F32, kind="ExternalInput").ap() for n, v in arrays.items()}
    out = nc.dram_tensor("out", (TOK, D), F32, kind="ExternalOutput").ap()
    build(nc, d["x"], (d["wa0"], d["wa1"]), (d["wax0"], d["wax1"]), (d["wb0"], d["wb1"]), d["wdown0"], d["w2t"],
          d["consts"], d["scales"], out)
    r = run_bass_kernel_spmd(nc, [{f"in_{n}": v for n, v in arrays.items()}], core_ids=[0])
    return r.results[0]["out"].reshape(4, 256, D)
```

```python
from contextlib import ExitStack

import concourse.bass as bass
from concourse import mybir

F32 = mybir.dt.float32
F32R = mybir.dt.float32r
BF16 = mybir.dt.bfloat16
ALU = mybir.AluOpType
ACT = mybir.ActivationFunctionType
AX_X = mybir.AxisListType.X

P = 128
D = 256
NC = D // P
TOK = 1024
TILES = TOK // P
DH = 128
PAIRS = 8
UNITS = 8 * PAIRS
HID = 1024
LN_EPS = 1e-5
RMS_EPS = 1e-6
ATTN_SCALE = 0.08838834764831845
ROPE_BASE = 10000.0
LOW = -3.0e38
MASKED = -1.0e30
WA = (1024, 1536)
WA_FFN = 2048
WB = 512
WB_FFN = 1024
FIRST_SLOT, LOOP_FROM, LOOP_STEP, LOOPS, LAST_SLOT = -5, 11, 16, 3, 70
FIRST_TAIL = UNITS - 8 + 7
TAIL_SLOT = UNITS - 4
TWO_OUTPUT_BANKS = UNITS - 6
HI_HI, HI_LO, LO_HI = (0, 0), (0, 1), (1, 0)
PASSES = (HI_HI, HI_LO, LO_HI)


def live(it, c):
    return it is not None or 0 <= c < UNITS


def need(eng, sem, it, c, per=1):
    if it is not None:
        eng.wait_ge(sem, it * (LOOP_STEP * per) + max(c, 1))
    elif c > 0:
        eng.wait_ge(sem, c)


def need_pairs(eng, sem, it, c, per_pair):
    if it is not None:
        eng.wait_ge(sem, it * (2 * per_pair) + c)
    elif c > 0:
        eng.wait_ge(sem, c)


def build(nc, x_in, wa, wax, wb, wdown0, w2t, consts, scales, out):
    with ExitStack() as ctx:
        def sb(name, shape, dt=F32):
            return ctx.enter_context(nc.sbuf_tensor(name, shape, dt))

        def sem(name):
            return ctx.enter_context(nc.semaphore(name))

        bank = [ctx.enter_context(nc.psum_tensor(f"bank{i}", [P, 512], F32)) for i in range(8)]
        S_BANK, PJ_BANK, TQ_BANK, PT_BANK, O_BANK, OP_BANK = 0, 2, 4, 5, 6, 7

        x = sb("x", [P, TILES, D])
        xT = [sb("xT_hi", [P, NC, TOK], F32R), sb("xT_lo", [P, NC, TOK], F32R)]
        xn = sb("xn", [P, 4, D])
        raw_a = sb("raw_a", [P, 2, 1536])
        raw_b = sb("raw_b", [P, 2, WB_FFN])
        a_w = [[sb(f"a_{part}{s}", [P, WA_FFN], F32R) for part in ("hi", "lo")] for s in range(2)]
        b_w = [[sb(f"b_{part}{s}", [P, WB_FFN], F32R) for part in ("hi", "lo")] for s in range(2)]
        qk = sb("qk", [P, 4, TOK])
        v = sb("v", [P, 2, TILES, 2 * DH])
        enc = [sb("enc_hi", [P, 2, TOK], F32R), sb("enc_lo", [P, 2, TOK], F32R)]
        scores = sb("scores", [P, 2, 384])
        probs = sb("probs", [P, 4, 384])
        probs_t = sb("probs_t", [P, 2, 384])
        rowmax = sb("rowmax", [P, 2, 2])
        negmax = sb("negmax", [P, 2, 2])
        rowsum = sb("rowsum", [P, 4, 2])
        rinv = sb("rinv", [P, 4, 2])
        squares = sb("squares", [P, 384])
        sumsq = sb("sumsq", [P, 2, 3])
        meansq = sb("meansq", [P, 2, 3])
        rms_r = sb("rms_r", [P, TILES, 3])
        rot_a = sb("rot_a", [P, 2, 384])
        rot_b = sb("rot_b", [P, 2, 384])
        cos_t = sb("cos_t", [P, 2, 3, DH])
        sin_t = sb("sin_t", [P, 2, 3, DH])
        cst = sb("cst", [P, 1536])
        scl = sb("scl", [P, 4, DH])
        ident = cst[:, 0:128]
        mask = [cst[:, 768:1152], cst[:, 1152:1536]]
        cos_c = cst[:, 256:512].rearrange("p (i d) -> p i d", i=2)
        sin_c = cst[:, 512:768].rearrange("p (i d) -> p i d", i=2)
        had = cst[:, 128:256]
        zero = sb("zero", [P, 1])
        neg_half = sb("neg_half", [P, TILES])
        ln_stats = sb("ln_stats", [P, 4, 6])
        ln_mv = sb("ln_mv", [P, TILES, 2])
        ln_ve = sb("ln_ve", [P, TILES])
        ln_r = sb("ln_r", [P, TILES])
        gate = sb("gate", [P, 2, 512])
        hid = qk[:, :, :].rearrange("p (b h) t -> p b (h t)", b=2).rearrange("p b (j t) -> p b j t", j=4)
        mag = v[:, 0, :, :].rearrange("p t d -> p (t d)").rearrange("p (j t) -> p j t", j=4)
        work = sb("work", [P, 2560])
        bits = work[:, :].bitcast(BF16).rearrange("p (n t) -> p n t", t=512)
        cmp, cnt = bits[:, 0:6, :], bits[:, 6:10, :]
        encf = [e[:, :, :].rearrange("p h t -> p (h t)").rearrange("p (j t) -> p j t", j=4) for e in enc]
        w2_a = sb("w2_a", [P, 8, D])
        w2_b = work[:, 0:8 * D].rearrange("p (a d) -> p a d", d=D)

        s_x = [sem(f"x_loaded{i}") for i in range(4)]
        s_ident, s_rope, s_mask = sem("identity_loaded"), sem("rotation_loaded"), sem("masks_loaded")
        s_scl, s_w2 = sem("scales_loaded"), sem("w2_loaded")
        s_zero, s_half, s_tab, s_scq = (sem(n) for n in ("zero_set", "half_set", "tables_made", "qscale_made"))
        ln = {n: sem("ln_" + n) for n in ("stats", "mv", "ve", "r", "xn", "turned", "hi", "lo")}
        names = ("scores", "max", "nb", "exp", "rinv", "pnorm", "pt", "ptev", "pv", "ehi", "elo", "op", "opadd",
                 "proj", "vproj", "qkev", "vev", "sq", "ss", "ms", "rp", "rot", "radd", "roped", "tq", "tqev",
                 "a0hi", "a0", "ahi", "a", "bhi", "b")
        at = [{n: sem(f"L{L}_{n}") for n in names} for L in range(2)]
        raw_as = [[sem(f"L{L}_raw_a{s}") for s in range(2)] for L in range(2)]
        raw_bs = [[sem(f"L{L}_raw_b{s}") for s in range(2)] for L in range(2)]
        fnames = ("whi", "w", "gate", "up", "silu", "h", "abs", "cmp", "hs", "hi", "lo", "lo23", "down", "xadd")
        ff = [{n: sem(f"F{f}_{n}") for n in fnames} for f in range(2)]
        s_bf, s_hadmm, s_hadev = (sem(n) for n in ("butterfly", "had_product", "w2_made"))
        s_out = sem("stored")

        def ffn_pieces(f):
            rest, main = WA_FFN - WA[f], WA[f]
            ps = [("x0", "a", 0, main + c, c, 10) for c in range(0, rest, 512)]
            ps += [("a9", "a", 1, c, c, 9) for c in range(0, main, 512)]
            ps += [("x1", "a", 1, main + c, c, 11) for c in range(0, rest, 512)]
            ps += [(f"b{s}", "b", s, c, c, 8 + s) for s in range(2) for c in (0, 512)]
            return ps

        pieces = [ffn_pieces(f) for f in range(2)]

        def pieces_until(f, last):
            return max(i + 1 for i, p in enumerate(pieces[f]) if p[0] == last)

        def ln_dve_bn(dve, st, t):
            nc.vector.bn_stats(ln_stats[:, t % 4, :], x[:, t, :]).then_inc(ln["stats"], 1)

        def ln_dve_aggr(dve, st, t):
            dve.wait_ge(ln["stats"], 8 * st + t + 1)
            nc.vector.bn_aggr(ln_mv[:, t, :], ln_stats[:, t % 4, :]).then_inc(ln["mv"], 1)

        def ln_dve_ve(dve, st, t):
            dve.wait_ge(ln["mv"], 8 * st + t + 1)
            nc.vector.tensor_scalar(ln_ve[:, t:t + 1], ln_mv[:, t, 1:2], LN_EPS, None, ALU.add).then_inc(ln["ve"], 1)

        def ln_dve_stats(dve, st, *tiles):
            for step in (ln_dve_bn, ln_dve_aggr, ln_dve_ve):
                for t in tiles:
                    step(dve, st, t)

        def ln_pool(pool, st, t):
            i = 8 * st + t
            pool.wait_ge(ln["ve"], i + 1)
            nc.gpsimd.tensor_tensor(ln_r[:, t:t + 1], ln_ve[:, t:t + 1], neg_half[:, 0:1], ALU.pow).then_inc(ln["r"], 1)

        def ln_dve_scale(dve, st, t):
            i = 8 * st + t
            dve.wait_ge(ln["r"], i + 1)
            if i >= 4:
                dve.wait_ge(ln["turned"], i - 3)
            nc.vector.tensor_scalar(xn[:, t % 4, :], x[:, t, :], ln_mv[:, t, 0:1], ln_r[:, t:t + 1],
                                    ALU.subtract, ALU.mult).then_inc(ln["xn"], 1)

        def ln_pe(pe, st, t, bk):
            i = 8 * st + t
            pe.wait_ge(ln["xn"], i + 1)
            for c in range(NC):
                mm = pe.transpose(bank[bk][:, c * P:(c + 1) * P], xn[:, t % 4, c * P:(c + 1) * P], ident)
            mm.then_inc(ln["turned"], 1)

        def ln_act(act, st, t, bk):
            i = 8 * st + t
            act.wait_ge(ln["turned"], i + 1)
            src = bank[bk][:, 0:D].rearrange("p (c t) -> p c t", c=NC)
            nc.scalar.copy(xT[0][:, :, t * P:(t + 1) * P], src).then_inc(ln["hi"], 1)

        def ln_dve_lo(dve, st, t, bk):
            i = 8 * st + t
            dve.wait_ge(ln["hi"], i + 1)
            src = bank[bk][:, 0:D].rearrange("p (c t) -> p c t", c=NC)
            nc.vector.tensor_tensor(xT[1][:, :, t * P:(t + 1) * P], src, xT[0][:, :, t * P:(t + 1) * P].bitcast(F32),
                                    ALU.subtract).then_inc(ln["lo"], 1)

        def output_bank(m):
            return bank[TQ_BANK if m > TWO_OUTPUT_BANKS and m % 2 else OP_BANK]

        def pe_scores(pe, L, it, c):
            s = at[L]
            if live(it, c):
                u = c % 8
                b, hh = u // 2, u % 2
                need(pe, s["max"], it, 2 * c - 2, 2)
                if L == 0:
                    need(pe, s["tqev"], it, c - hh + 2)
                    q, k = hh, 2
                else:
                    need(pe, s["qkev"], it, c - u + 4 * (b // 2) + 2 * hh + 2)
                    q, k = 2 * hh, 2 * hh + 1
                ps = bank[S_BANK + c % 2]
                t0 = b * D
                pe.matmul(ps[:, 0:128], qk[:, q, t0:t0 + 128], qk[:, k, t0:t0 + 128], start=True, stop=True)
                pe.matmul(ps[:, 128:384], qk[:, q, t0 + 128:t0 + 256], qk[:, k, t0:t0 + 256],
                          start=True, stop=True).then_inc(s["scores"], 1)

        def pe_slot(pe, L, it, c):
            s = at[L]
            pe_scores(pe, L, it, c if c < TAIL_SLOT else c + 1)
            m = c + 5
            if live(it, m):
                t, slot = m % 8, (m // 8) % 2
                if t == 0:
                    if it is None and m == 0:
                        pe.wait_ge(s["a0"], 1 if L == 0 else 4)
                    else:
                        need_pairs(pe, s["a"], it, 4 * (m // 8), 4)
                if it is None and m < 8:
                    ready = m + 1 if L == 0 else 4 * (m // 4 + 1)
                    pe.wait_ge(ln["lo"], 16 * L + ready)
                ps = bank[PJ_BANK + m % 2]
                if L == 0:
                    need(pe, s["rot"], it, m - 1)
                    for i, (g, (l, r)) in enumerate([(g, p) for g in range(NC) for p in PASSES]):
                        mm = pe.matmul(ps[:, :], xT[l][:, g, t * P:(t + 1) * P], a_w[slot][r][:, g * 512:(g + 1) * 512],
                                       start=i == 0, stop=i == 5)
                else:
                    half, w = t // 4, t % 4
                    need(pe, s["qkev"], it, m - 1)
                    for i, (g, (l, r)) in enumerate([(g, p) for g in range(NC) for p in PASSES]):
                        mm = pe.matmul(ps[:, :], a_w[slot][l][:, g * 768 + w * P:g * 768 + (w + 1) * P],
                                       xT[r][:, g, half * 512:(half + 1) * 512], start=i == 0, stop=i == 5)
                mm.then_inc(s["proj"], 1)
            m = c - 6
            if live(it, m):
                t, slot = m % 8, (m // 8) % 2
                need(pe, s["elo"], it, m - t % 2 + 2)
                if t == 0:
                    need_pairs(pe, s["b"], it, 4 * (m // 8 + 1), 4)
                if m == TWO_OUTPUT_BANKS + 1:
                    pe.wait_ge(s["tqev" if L == 0 else "vev"], UNITS)
                elif m > TWO_OUTPUT_BANKS:
                    pe.wait_ge(s["opadd"], m - 1)
                else:
                    need(pe, s["opadd"], it, m)
                for i, (h, (l, r)) in enumerate([(h, p) for h in range(2) for p in PASSES]):
                    mm = pe.matmul(output_bank(m)[:, 0:D], enc[l][:, h, t * P:(t + 1) * P],
                                   b_w[slot][r][:, h * D:(h + 1) * D], start=i == 0, stop=i == 5)
                mm.then_inc(s["op"], 1)
            if L == 1:
                m = c + 5
                if live(it, m):
                    t, slot = m % 8, (m // 8) % 2
                    if it is None and m < 8:
                        pe.wait_ge(ln["lo"], 16 + 4 * (m // 4 + 1))
                    need(pe, s["vev"], it, m)
                    for i, (g, (l, r)) in enumerate([(g, p) for g in range(NC) for p in PASSES]):
                        mm = pe.matmul(bank[TQ_BANK][:, 0:D], xT[l][:, g, t * P:(t + 1) * P],
                                       a_w[slot][r][:, g * 768 + 512:(g + 1) * 768], start=i == 0, stop=i == 5)
                    mm.then_inc(s["vproj"], 1)
            m = c - 2
            if live(it, m):
                need(pe, s["pnorm"], it, 2 * m + 2, 2)
                need(pe, s["ptev"], it, m)
                for j in range(3):
                    mm = pe.transpose(bank[PT_BANK][:, j * P:(j + 1) * P], probs[:, m % 4, j * P:(j + 1) * P], ident)
                mm.then_inc(s["pt"], 1)
            m = c - 3
            if live(it, m):
                u = m % 8
                b, hh = u // 2, u % 2
                vc = 0 if L == 0 else hh * DH
                need(pe, s["ptev"], it, m + 1)
                need(pe, s["vev"], it, m - hh + 2)
                need(pe, s["elo"], it, m)
                pe.matmul(bank[O_BANK][:, 0:256], v[:, m // 8 % 2, 2 * b, vc:vc + DH], probs_t[:, m % 2, 0:256],
                          start=True, stop=False, skip_group_check=True)
                pe.matmul(bank[O_BANK][:, 128:256], v[:, m // 8 % 2, 2 * b + 1, vc:vc + DH], probs_t[:, m % 2, 256:384],
                          start=False, stop=True, skip_group_check=True).then_inc(s["pv"], 1)
            if L == 0:
                m = c + 3
                if live(it, m):
                    need(pe, s["roped"], it, m + 1)
                    need(pe, s["tqev"], it, m)
                    for j in range(3):
                        mm = pe.transpose(bank[TQ_BANK][:, j * P:(j + 1) * P], rot_a[:, m % 2, j * P:(j + 1) * P], ident)
                    mm.then_inc(s["tq"], 1)
            if c == TAIL_SLOT - 1:
                pe_scores(pe, L, it, TAIL_SLOT)

        def act_slot(act, L, it, c):
            s = at[L]
            m = c - 3
            if live(it, m):
                need(act, s["pt"], it, m + 1)
                need(act, s["pv"], it, m - 1)
                nc.scalar.copy(probs_t[:, m % 2, :], bank[PT_BANK][:, 0:384]).then_inc(s["ptev"], 1)
            m = c - 4
            if live(it, m):
                u = m % 8
                b, hh = u // 2, u % 2
                need(act, s["pv"], it, m + 1)
                need(act, s["op"], it, m - hh - 6)
                nc.scalar.copy(enc[0][:, hh, b * D:(b + 1) * D], bank[O_BANK][:, 0:D]).then_inc(s["ehi"], 1)
            m = c + 4
            if live(it, m):
                t = m % 8
                need(act, s["proj"], it, m + 1)
                if L == 0:
                    need(act, s["ss"], it, m)
                    nc.scalar.activation(squares[:, :], bank[PJ_BANK + m % 2][:, 0:384], ACT.Square).then_inc(s["sq"], 1)
                    need(act, s["pv"], it, m - t % 2 - 14)
                    nc.scalar.copy(v[:, m // 8 % 2, t, 0:DH], bank[PJ_BANK + m % 2][:, 384:512]).then_inc(s["vev"], 1)
                else:
                    half, w = t // 4, t % 4
                    need(act, s["scores"], it, m - t + 4 * half - 4)
                    if it is None and m in (0, 2):
                        act.wait_ge(ff[0]["lo"], 10 + m)
                        act.wait_ge(ff[0]["lo23"], 2 + m)
                    nc.scalar.copy(qk[:, w, half * 512:(half + 1) * 512], bank[PJ_BANK + m % 2][:, :]).then_inc(s["qkev"], 1)
                    need(act, s["vproj"], it, m + 1)
                    need(act, s["pv"], it, m - t % 2 - 14)
                    if it is None and m == 0:
                        act.wait_ge(ff[0]["cmp"], 24)
                    nc.scalar.copy(v[:, m // 8 % 2, t, :], bank[TQ_BANK][:, 0:D]).then_inc(s["vev"], 1)
            if L == 0:
                m = c + 2
                if live(it, m):
                    t = m % 8
                    need(act, s["tq"], it, m + 1)
                    need(act, s["scores"], it, m - t % 2 - 6)
                    nc.scalar.copy(qk[:, 0:3, t * P:(t + 1) * P],
                                   bank[TQ_BANK][:, 0:384].rearrange("p (a t) -> p a t", a=3)).then_inc(s["tqev"], 1)
            if live(it, c):
                u = c % 8
                b, hh = u // 2, u % 2
                need(act, s["nb"], it, c + 1)
                need(act, s["pt"], it, c - 3)
                for r, (c0, c1) in enumerate(((0, 128), (128, 384))):
                    scale = rms_r[:, 2 * b + r, hh:hh + 1] if L == 0 else float(DH) ** -0.5
                    nc.scalar.activation(probs[:, c % 4, c0:c1], scores[:, c % 2, c0:c1], ACT.Exp,
                                         bias=negmax[:, c % 2, r:r + 1], scale=scale,
                                         accum_out=rowsum[:, c % 4, r:r + 1]).then_inc(s["exp"], 1)

        def dve_normalise(dve, L, it, c):
            s, m = at[L], c - 1
            if live(it, m):
                need(dve, s["exp"], it, 2 * m + 2, 2)
                nc.vector.reciprocal(rinv[:, m % 4, :], rowsum[:, m % 4, :]).then_inc(s["rinv"], 1)
                need(dve, s["rinv"], it, m + 1)
                for r, (c0, c1) in enumerate(((0, 128), (128, 384))):
                    nc.vector.tensor_scalar(probs[:, m % 4, c0:c1], probs[:, m % 4, c0:c1], rinv[:, m % 4, r:r + 1], None,
                                            ALU.mult).then_inc(s["pnorm"], 1)

        def dve_residual(dve, L, it, c):
            s, m = at[L], c - 7
            if live(it, m):
                need(dve, s["op"], it, m + 1)
                nc.vector.tensor_tensor(x[:, m % 8, :], output_bank(m)[:, 0:D], x[:, m % 8, :], ALU.add).then_inc(s["opadd"], 1)

        def dve_enc_lo(dve, L, it, c):
            s, m = at[L], c - 4
            if live(it, m):
                w = m % 8
                need(dve, s["ehi"], it, m + 1)
                dst = slice((w // 2) * D, (w // 2 + 1) * D)
                nc.vector.tensor_tensor(enc[1][:, w % 2, dst], bank[O_BANK][:, 0:D], enc[0][:, w % 2, dst].bitcast(F32),
                                        ALU.subtract).then_inc(s["elo"], 1)

        def dve_scores_wait(dve, L, it, c):
            s = at[L]
            if live(it, c):
                need(dve, s["scores"], it, c + 1)
                need(dve, s["exp"], it, 2 * c - 2, 2)

        def dve_maxima(dve, L, it, c):
            s = at[L]
            if live(it, c):
                b, hh = c % 8 // 2, c % 2
                for r, (c0, c1) in enumerate(((0, 128), (128, 384))):
                    nc.vector.tensor_tensor_reduce(out=scores[:, c % 2, c0:c1], in0=bank[S_BANK + c % 2][:, c0:c1],
                                                   in1=mask[L][:, c0:c1], scale=1.0, scalar=LOW, op0=ALU.add, op1=ALU.max,
                                                   accum_out=rowmax[:, c % 2, r:r + 1]).then_inc(s["max"], 1)
                need(dve, s["max"], it, 2 * c + 2, 2)
                if L == 0:
                    need(dve, s["rp"], it, c - hh + 2)
                    nc.vector.scalar_tensor_tensor(out=negmax[:, c % 2, :], in0=rowmax[:, c % 2, :], scalar=-1.0,
                                                   in1=rms_r[:, 2 * b:2 * b + 2, hh], op0=ALU.mult,
                                                   op1=ALU.mult).then_inc(s["nb"], 1)
                else:
                    nc.vector.tensor_scalar(negmax[:, c % 2, :], rowmax[:, c % 2, :], -float(DH) ** -0.5, None,
                                            ALU.mult).then_inc(s["nb"], 1)

        def dve_slot(dve, L, it, c):
            s = at[L]
            if c < TAIL_SLOT:
                dve_normalise(dve, L, it, c)
                dve_residual(dve, L, it, c)
                dve_scores_wait(dve, L, it, c)
                dve_enc_lo(dve, L, it, c)
                dve_maxima(dve, L, it, c)
            else:
                dve_scores_wait(dve, L, it, c)
                dve_maxima(dve, L, it, c)
                dve_normalise(dve, L, it, c)
                dve_residual(dve, L, it, c)
                dve_enc_lo(dve, L, it, c)
            m = c + 4
            if live(it, m):
                t = m % 8
                if L == 0:
                    ps = bank[PJ_BANK + m % 2]
                    need(dve, s["sq"], it, m + 1)
                    nc.vector.reduce_sum(sumsq[:, m % 2, :], squares[:, :].rearrange("p (a d) -> p a d", a=3),
                                         AX_X).then_inc(s["ss"], 1)
                    need(dve, s["vev"], it, m + 1)
                    need(dve, s["tq"], it, m - 1)
                    nc.vector.tensor_tensor(rot_a[:, m % 2, :], ps[:, 0:384],
                                            cos_t[:, t % 2, :, :].rearrange("p a d -> p (a d)"), ALU.mult)
                    need(dve, s["ss"], it, m + 1)
                    need(dve, s["rp"], it, m - 1)
                    nc.vector.tensor_scalar(meansq[:, m % 2, :], sumsq[:, m % 2, :], 1.0 / DH, RMS_EPS,
                                            ALU.mult, ALU.add).then_inc(s["ms"], 1)
                    need(dve, s["radd"], it, m - 1)
                    nc.vector.tensor_tensor(
                        rot_b[:, m % 2, :].rearrange("p (a h d) -> p a h d", a=3, h=2),
                        ps[:, 0:384].rearrange("p (a h d) -> p a h d", a=3, h=2)[:, :, ::-1, :],
                        sin_t[:, t % 2, :, :].rearrange("p a (h d) -> p a h d", h=2), ALU.mult).then_inc(s["rot"], 1)

        def split(hi, lo, src, eng, s_hi, wait, s_lo):
            nc.gpsimd.tensor_tensor(hi, src, zero[:, 0:1].broadcast_to(list(src.shape)), ALU.add).then_inc(s_hi, 1)
            wait()
            nc.gpsimd.tensor_tensor(lo, src, hi.bitcast(F32), ALU.subtract).then_inc(s_lo, 1)

        def pool_slot(pool, L, it, c):
            s = at[L]
            if L == 0:
                m = c + 3
                if live(it, m):
                    t = m % 8
                    need(pool, s["ms"], it, m + 1)
                    need(pool, s["exp"], it, 2 * (m - t % 2) - 12, 2)
                    nc.gpsimd.tensor_tensor(rms_r[:, t, :], meansq[:, m % 2, :], neg_half[:, 0:3], ALU.pow).then_inc(s["rp"], 1)
                    need(pool, s["rot"], it, m + 1)
                    nc.gpsimd.tensor_tensor(rot_a[:, m % 2, :], rot_a[:, m % 2, :], rot_b[:, m % 2, :],
                                            ALU.add).then_inc(s["radd"], 1)
                    need(pool, s["radd"], it, m + 1)
                    need(pool, s["rp"], it, m + 1)
                    nc.gpsimd.tensor_tensor(rot_a[:, m % 2, 256:384], rot_a[:, m % 2, 256:384],
                                            rms_r[:, t, 2:3].broadcast_to([P, DH]), ALU.mult).then_inc(s["roped"], 1)
            m = c + 5
            if (it is not None or (8 if L == 0 else 0) <= m < 64) and m % 2 == 0:
                pair, part = m // 8 + 1, m % 8 // 2
                w, slot = WA[L] // 4, pair % 2
                if part == 0:
                    need_pairs(pool, raw_as[L][slot], it, 16 * (pair // 2 + 1), 8)
                    need(pool, s["proj"], it, 8 * (pair - 1))
                    if L == 1:
                        need(pool, s["vproj"], it, 8 * (pair - 1))
                    if L == 1 and it is None and pair == 1:
                        pool.wait_ge(ff[0]["up"], 16)
                cs = slice(part * w, (part + 1) * w)
                done = 4 * (pair - 1) + part + 1
                split(a_w[slot][0][:, cs], a_w[slot][1][:, cs], raw_a[:, slot, cs], pool, s["ahi"],
                      lambda: need_pairs(pool, s["ahi"], it, done, 4), s["a"])
            m = c - 6
            if (it is not None or -8 <= m < 56) and m % 2 == 0:
                pair, part = m // 8 + 1, m % 8 // 2
                w, slot = WB // 4, pair % 2
                if part == 0:
                    need_pairs(pool, raw_bs[L][slot], it, 16 * (pair // 2 + 1), 8)
                    need(pool, s["op"], it, 8 * (pair - 1))
                    if L == 1 and it is None and pair == 0:
                        pool.wait_ge(ff[0]["down"], 12)
                    if L == 1 and it is None and pair == 1:
                        pool.wait_ge(ff[0]["down"], 16)
                cs = slice(part * w, (part + 1) * w)
                done = 4 * pair + part + 1
                split(b_w[slot][0][:, cs], b_w[slot][1][:, cs], raw_b[:, slot, cs], pool, s["bhi"],
                      lambda: need_pairs(pool, s["bhi"], it, done, 4), s["b"])

        def slots(eng, L, body, head, tail):
            for c in range(FIRST_SLOT, LOOP_FROM):
                body(eng, L, None, c)
                head(c)
            with eng.Fori(0, LOOPS) as it:
                for j in range(LOOP_STEP):
                    body(eng, L, it, LOOP_FROM + j)
            for c in range(LOOP_FROM + LOOP_STEP * LOOPS, LAST_SLOT + 1):
                body(eng, L, None, c)
                tail(c - FIRST_TAIL)

        def pe_gate_up(pe, f, k, tiles=range(4)):
            s, L = ff[f], at[f]
            th, t = k // 2, k % 2
            base = 16 * f + 8
            for j in tiles:
                i = 4 * k + j
                r = i % 3
                if j == 0:
                    pe.wait_ge(ln["lo"], base + 4 * (th + 1))
                    if k < 2:
                        if k == 0:
                            pe.wait_ge(L["a"], 32)
                        pe.wait_ge(s["w"], pieces_until(f, "x0" if t == 0 else "x1"))
                if i >= 3:
                    pe.wait_ge(s["silu"], i - 2)
                    pe.wait_ge(s["h"], i - 2)
                elif i == 0:
                    pe.wait_ge(L["max"], 2 * UNITS)
                    if f == 1:
                        pe.wait_ge(s_hadev, 4)
                elif i == 1:
                    pe.wait_ge(L["rot" if f == 0 else "qkev"], UNITS)
                else:
                    pe.wait_ge(L["ptev"], UNITS)
                    pe.wait_ge(ln["lo"], base + 4)
                for up in range(2):
                    ps = bank[2 * r + up]
                    for q, (g, (l, rr)) in enumerate([(g, p) for g in range(NC) for p in PASSES]):
                        c0 = g * HID + up * 512 + j * P
                        mm = pe.matmul(ps[:, :], a_w[t][l][:, c0:c0 + P], xT[rr][:, g, th * 512:(th + 1) * 512],
                                       start=q == 0, stop=q == 5)
                    mm.then_inc(s["up" if up else "gate"], 1)
                if k == 0:
                    for tile in ((4,), (5, 6), (7,), ())[j]:
                        if tile == 4:
                            pe.wait_ge(L["elo"], UNITS)
                        elif tile == 5:
                            pe.wait_ge(L["opadd"], UNITS)
                        else:
                            pe.wait_ge(ln["lo"], base + tile - 1)
                        ln_pe(pe, 2 * f + 1, tile, 6 + tile % 2)

        def pe_down(pe, f, k, tiles=range(4)):
            s, L = ff[f], at[f]
            t = k % 2
            for tt in tiles:
                d = 4 * k + tt
                if tt == 0:
                    pe.wait_ge(s["hi"], 4 * k + 4)
                    if f == 0 and k >= 2:
                        pe.wait_ge(s["lo"], 2 * k + 6)
                        pe.wait_ge(s["lo23"], 2 * k - 2)
                    else:
                        pe.wait_ge(s["lo"], 4 * k + 4)
                    if k < 2:
                        pe.wait_ge(s["w"], pieces_until(f, f"b{t}"))
                if d < 2:
                    pe.wait_ge(ln["lo"], 16 * f + 16)
                if d >= 2:
                    pe.wait_ge(s["xadd"], d - 1)
                for q, (j, (l, r)) in enumerate([(j, p) for j in range(4) for p in PASSES]):
                    mm = pe.matmul(bank[6 + d % 2][:, 0:D], encf[l][:, j, tt * P:(tt + 1) * P],
                                   b_w[t][r][:, j * D:(j + 1) * D], start=q == 0, stop=q == 11)
                mm.then_inc(s["down"], 1)

        def down_bank(f, d):
            return (bank[6], bank[7], *((bank[0], bank[1]) if f == 0 else (bank[2], bank[3])))[d % (2 if d < 12 else 4)]

        def pe_last_down(pe, f):
            s = ff[f]
            pe.wait_ge(s["xadd"], 12)
            pe.wait_ge(s["h"], 16 if f == 0 else 14)
            for tiles in ((0, 1), (2, 3)) if f == 0 else (range(4),):
                for j in range(4):
                    pe.wait_ge(s["hi"], 12 + j + 1)
                    if f == 1:
                        pe.wait_ge(s["lo"], 12 + j + 1)
                    elif j < 2:
                        pe.wait_ge(s["lo"], 10 + j + 1)
                    else:
                        pe.wait_ge(s["lo23"], j + 1)
                    for tt in tiles:
                        for q, (l, r) in enumerate(PASSES):
                            mm = pe.matmul(down_bank(f, 12 + tt)[:, 0:D], encf[l][:, j, tt * P:(tt + 1) * P],
                                           b_w[1][r][:, j * D:(j + 1) * D], start=j == 0 and q == 0, stop=j == 3 and q == 2)
                        if j == 3:
                            mm.then_inc(s["down"], 1)

        def pe_hadamard(pe, q):
            pe.wait_ge(at[1]["max"], 2 * UNITS)
            pe.wait_ge(s_bf, 6)
            if q >= 2:
                pe.wait_ge(s_hadev, q - 1)
            pe.matmul(bank[S_BANK + q % 2][:, :], had, w2_b[:, 2 * q:2 * q + 2, :].rearrange("p a d -> p (a d)"),
                      start=True, stop=True).then_inc(s_hadmm, 1)

        LN2_BANK = (2, 3, 4, 5, 6, 7, 0, 1)

        def pe_ffn0(pe):
            pe_gate_up(pe, 0, 0)
            pe_gate_up(pe, 0, 1)
            pe_gate_up(pe, 0, 2, (0, 1, 2))
            pe_down(pe, 0, 0)
            pe_gate_up(pe, 0, 2, (3,))
            pe_gate_up(pe, 0, 3, (0, 1))
            pe_down(pe, 0, 1)
            pe_gate_up(pe, 0, 3, (2, 3))
            for t in range(4):
                pe.wait_ge(ff[0]["h"], 14 + t // 2)
                ln_pe(pe, 2, t, LN2_BANK[t])
            pe_down(pe, 0, 2)

        def pe_ffn1(pe):
            pe_gate_up(pe, 1, 0)
            for k in range(1, 4):
                pe_gate_up(pe, 1, k, (0, 1))
                pe_down(pe, 1, k - 1)
                pe_gate_up(pe, 1, k, (2, 3))
            pe_last_down(pe, 1)

        def act_silu(act, f, i):
            s = ff[f]
            act.wait_ge(s["gate"], i + 1)
            if i >= 2:
                act.wait_ge(s["h"], i - 1)
            nc.scalar.activation(gate[:, i % 2, :], bank[2 * (i % 3)][:, :], ACT.Silu).then_inc(s["silu"], 1)

        def act_ln_gate(act, f):
            st = 2 * f + 1
            ln_act(act, st, 4, 6)
            act_silu(act, f, 0)
            ln_act(act, st, 5, 7)
            ln_act(act, st, 6, 6)
            act_silu(act, f, 1)
            ln_act(act, st, 7, 7)
            act_silu(act, f, 2)
            act_silu(act, f, 3)

        def act_hi(act, f, k, tiles=range(4)):
            s = ff[f]
            if k == 0:
                act.wait_ge(at[f]["op"], UNITS)
            else:
                act.wait_ge(s["down"], 4 * k)
            for j in tiles:
                act.wait_ge(s["hs" if f == 0 else "h"], 4 * k + j + 1)
                nc.scalar.copy(encf[0][:, j, :], hid[:, k % 2, j, :]).then_inc(s["hi"], 1)

        def act_hadamard(act, q):
            act.wait_ge(s_hadmm, q + 1)
            nc.scalar.mul(w2_a[:, 2 * q:2 * q + 2, :].rearrange("p a d -> p (a d)"), bank[S_BANK + q % 2][:, :],
                          float(HID) ** -0.5).then_inc(s_hadev, 1)

        def act_abs(act, i):
            k, j = i // 4, i % 4
            act.wait_ge(ff[0]["h"], i + 1)
            if i == 0:
                act.wait_ge(at[0]["pv"], UNITS)
            elif k and j == 0:
                act.wait_ge(ff[0]["cmp"], 6 * k)
            nc.scalar.activation(mag[:, j, :], hid[:, k % 2, j, :], ACT.Abs).then_inc(ff[0]["abs"], 1)

        def act_ffn0(act):
            act_ln_gate(act, 0)
            for i in range(4):
                act_abs(act, i)
            for k in range(3):
                i = 4 * (k + 1)
                act_silu(act, 0, i)
                act_silu(act, 0, i + 1)
                act_silu(act, 0, i + 2)
                act_abs(act, i)
                act_abs(act, i + 1)
                if k == 2:
                    act_hi(act, 0, k)
                act_silu(act, 0, i + 3)
                act_abs(act, i + 2)
                if k < 2:
                    act_hi(act, 0, k)
                act_abs(act, i + 3)
            for t in range(4):
                ln_act(act, 2, t, LN2_BANK[t])

        def act_ffn1(act):
            act_ln_gate(act, 1)
            for k in range(3):
                act_hi(act, 1, k)
                act_silu(act, 1, 4 * k + 4)
                act_silu(act, 1, 4 * k + 5)
                if k == 2:
                    act_hi(act, 1, 3, (0, 1))
                act_silu(act, 1, 4 * k + 6)
                if k == 2:
                    act_hi(act, 1, 3, (2,))
                act_silu(act, 1, 4 * k + 7)
            act_hi(act, 1, 3, (3,))

        def dve_hidden(dve, f, i):
            s = ff[f]
            k, j = i // 4, i % 4
            dve.wait_ge(s["silu"], i + 1)
            dve.wait_ge(s["up"], i + 1)
            if i == 0:
                dve.wait_ge(at[f]["scores"], UNITS)
            if k >= 2:
                dve.wait_ge(s["hi"], 4 * k - 8 + j + 1)
                dve.wait_ge(s["lo"], 4 * k - 8 + j + 1)
            nc.vector.tensor_tensor(hid[:, k % 2, j, :], bank[2 * (i % 3) + 1][:, :], gate[:, i % 2, :],
                                    ALU.mult).then_inc(s["h"], 1)

        def dve_ln_hidden(dve, f):
            st = 2 * f + 1
            ln_dve_scale(dve, st, 7)
            ln_dve_lo(dve, st, 4, 6)
            dve_hidden(dve, f, 0)
            ln_dve_lo(dve, st, 5, 7)
            ln_dve_lo(dve, st, 6, 6)
            dve_hidden(dve, f, 1)
            ln_dve_lo(dve, st, 7, 7)
            dve_hidden(dve, f, 2)
            dve_hidden(dve, f, 3)

        def dve_xadd(dve, f, k, tt):
            s = ff[f]
            d, t = 4 * k + tt, 4 * (k // 2) + tt
            dve.wait_ge(s["down"], d + 1)
            nc.vector.tensor_tensor(x[:, t, :], down_bank(f, d)[:, 0:D], x[:, t, :], ALU.add).then_inc(s["xadd"], 1)
            if f == 0 and k == 1:
                dve.wait_ge(s["xadd"], d + 1)
                ln_dve_stats(dve, 2, t)

        def dve_compare(dve, k, n):
            s = ff[0]
            a, b = ((0, 1), (0, 2), (1, 2), (0, 3), (1, 3), (2, 3))[n]
            dve.wait_ge(s["abs"], 4 * k + b + 1)
            nc.vector.tensor_tensor(cmp[:, n, :], mag[:, a, :], mag[:, b, :], ALU.is_ge).then_inc(s["cmp"], 1)

        s_cnt = sem("kept_counts")

        C01, C02, C12, C03, C13, C23 = range(6)
        KEEP = ((C01, C02, C03, ALU.add, ALU.is_ge, 1.5), (C12, C13, C01, ALU.subtract, ALU.is_ge, 0.5),
                (C02, C12, C23, ALU.subtract, ALU.is_lt, 0.5), (C03, C13, C23, ALU.add, ALU.is_lt, 1.5))

        def dve_count(dve, k, step):
            for j, (a, b, c, op, _, _) in enumerate(KEEP):
                if step == 0:
                    if j == 0:
                        dve.wait_ge(ff[0]["cmp"], 6 * k + 6)
                    nc.vector.tensor_tensor(cnt[:, j, :], cmp[:, a, :], cmp[:, b, :], ALU.add).then_inc(s_cnt, 1)
                else:
                    dve.wait_ge(s_cnt, 8 * k + j + 1)
                    nc.vector.tensor_tensor(cnt[:, j, :], cnt[:, j, :], cmp[:, c, :], op).then_inc(s_cnt, 1)

        def dve_keep(dve, k, tiles=range(4)):
            for j in tiles:
                keep, than = KEEP[j][4:]
                dve.wait_ge(s_cnt, 8 * k + 4 + j + 1)
                h = hid[:, k % 2, j, :]
                nc.vector.scalar_tensor_tensor(out=h, in0=cnt[:, j, :], scalar=than, in1=h, op0=keep,
                                               op1=ALU.mult).then_inc(ff[0]["hs"], 1)

        def dve_lo23(dve, k):
            for j in (2, 3):
                dve.wait_ge(ff[0]["hi"], 4 * k + j + 1)
                nc.vector.tensor_tensor(encf[1][:, j, :], hid[:, k % 2, j, :], encf[0][:, j, :].bitcast(F32),
                                        ALU.subtract).then_inc(ff[0]["lo23"], 1)

        def dve_ffn0(dve):
            dve_ln_hidden(dve, 0)
            for k in range(3):
                i = 4 * (k + 1)
                for n in range(4):
                    dve_compare(dve, k, n)
                dve_hidden(dve, 0, i)
                for n in range(4, 6):
                    dve_compare(dve, k, n)
                dve_count(dve, k, 0)
                dve_hidden(dve, 0, i + 1)
                dve_count(dve, k, 1)
                if k == 2:
                    for tt in range(4):
                        dve_xadd(dve, 0, 1, tt)
                        dve_keep(dve, 2, (tt,))
                dve_hidden(dve, 0, i + 2)
                if k == 1:
                    for tt in range(4):
                        dve_xadd(dve, 0, 0, tt)
                if k < 2:
                    dve_keep(dve, k)
                else:
                    for t in range(4):
                        ln_dve_scale(dve, 2, t)
                    dve_lo23(dve, 2)
                dve_hidden(dve, 0, i + 3)
            for t in range(4):
                ln_dve_lo(dve, 2, t, LN2_BANK[t])
            for n in range(6):
                if n % 2 == 0:
                    dve_xadd(dve, 0, 2, n // 2)
                dve_compare(dve, 3, n)
            dve_xadd(dve, 0, 2, 3)
            dve_count(dve, 3, 0)

        def dve_ffn1_lo(dve, k, tiles=range(4)):
            s = ff[1]
            for j in tiles:
                dve.wait_ge(s["hi"], 4 * k + j + 1)
                nc.vector.tensor_tensor(encf[1][:, j, :], hid[:, k % 2, j, :], encf[0][:, j, :].bitcast(F32),
                                        ALU.subtract).then_inc(s["lo"], 1)

        def dve_ffn1(dve):
            dve_ln_hidden(dve, 1)
            for k in range(3):
                dve_ffn1_lo(dve, k)
                dve_hidden(dve, 1, 4 * k + 4)
                dve_hidden(dve, 1, 4 * k + 5)
                for tt in range(4):
                    dve_xadd(dve, 1, k, tt)
                if k == 2:
                    dve_ffn1_lo(dve, 3, (0, 1))
                dve_hidden(dve, 1, 4 * k + 6)
                if k == 2:
                    dve_ffn1_lo(dve, 3, (2,))
                dve_hidden(dve, 1, 4 * k + 7)
            dve_ffn1_lo(dve, 3, (3,))
            for tt in range(4):
                dve_xadd(dve, 1, 3, tt)

        def pool_piece(pool, f, n):
            what, ring, slot, col, src, load = pieces[f][n]
            s, L = ff[f], at[f]
            if ring == "a":
                pool.wait_ge(raw_as[f][slot], 16 * (load // 2 + 1))
                if what == "a9":
                    pool.wait_ge(L["proj"], UNITS)
                    if f == 1:
                        pool.wait_ge(L["vproj"], UNITS)
                source, dst = raw_a[:, slot, src:src + 512], a_w[slot]
            else:
                pool.wait_ge(L["op"], UNITS - 8 * (1 - slot))
                if f == 0:
                    pool.wait_ge(raw_bs[0][slot], 16 * (load // 2 + 1))
                    source = raw_b[:, slot, src:src + 512]
                else:
                    pool.wait_ge(s_hadev, 4)
                    a = 4 * slot + src // D
                    source = w2_a[:, a:a + 2, :].rearrange("p a d -> p (a d)")
                dst = b_w[slot]
            split(dst[0][:, col:col + 512], dst[1][:, col:col + 512], source, pool, s["whi"],
                  lambda: pool.wait_ge(s["whi"], n + 1), s["w"])

        def pool_tail(pool, f):
            def tail(t):
                n = t + FIRST_TAIL - (LOOP_FROM + LOOP_STEP * LOOPS)
                if n < 4:
                    pool_piece(pool, f, n)
                if t >= 0:
                    ln_pool(pool, 2 * f + 1, t)
            return tail

        def pool_head(c):
            if c == -3:
                for t in range(4, 8):
                    ln_pool(nc.gpsimd, 2, t)
            if c == 1:
                nc.gpsimd.wait_ge(s_w2, 16)
                nc.gpsimd.wait_ge(ff[0]["hs"], 16)
            if 1 <= c <= 6:
                n = c - 1
                src, dst = ((w2_a, w2_b), (w2_b, w2_a))[n // 2 % 2]
                h = 4 >> n // 2
                a = src[:, :, :].rearrange("p (g s h) d -> p g s (h d)", s=2, h=h)
                b = dst[:, :, :].rearrange("p (g s h) d -> p g s (h d)", s=2, h=h)
                if n >= 2:
                    nc.gpsimd.wait_ge(s_bf, 2 * (n // 2))
                nc.gpsimd.tensor_tensor(b[:, :, n % 2, :], a[:, :, 0, :], a[:, :, 1, :],
                                        (ALU.add, ALU.subtract)[n % 2]).then_inc(s_bf, 1)

        def pool_lo(pool, k):
            s = ff[0]
            for j in range(4 if k < 2 else 2):
                pool.wait_ge(s["hi"], 4 * k + j + 1)
                pool.wait_ge(s["down"], 4 * k) if k else pool.wait_ge(at[0]["op"], UNITS)
                nc.gpsimd.tensor_tensor(encf[1][:, j, :], hid[:, k % 2, j, :], encf[0][:, j, :].bitcast(F32),
                                        ALU.subtract).then_inc(s["lo"], 1)

        block = ctx.enter_context(nc.Block())

        @block.sync
        def _(sp):
            x_v = x_in.rearrange("(t p) d -> p t d", p=P)
            for i in range(4):
                sp.dma_start(x[:, 2 * i:2 * i + 2, :], x_v[:, 2 * i:2 * i + 2, :]).then_inc(s_x[i], 16)
            for L in range(2):
                s = at[L]

                def load(it, pair):
                    slot = pair % 2
                    if L == 1 and it is None and pair < 2:
                        sp.wait_ge(ff[0]["w"], pieces_until(0, f"x{pair}"))
                        sp.wait_ge(ff[0]["w"], pieces_until(0, f"b{pair}"))
                    if it is None and pair == 2:
                        sp.wait_ge(s["a0"], 1 if L == 0 else 4)
                    else:
                        need_pairs(sp, s["a"], it, 4 * (pair - 2), 4)
                    n = pair if it is None else it * 2 + pair
                    if not (L == 0 and it is None and pair == 0):
                        sp.dma_start(raw_a[:, slot, 0:WA[L]], wa[L][n]).then_inc(raw_as[L][slot], 16)
                    if it is not None or pair < PAIRS:
                        need_pairs(sp, s["b"], it, 4 * (pair - 1), 4)
                        sp.dma_start(raw_b[:, slot, 0:WB], wb[L][n]).then_inc(raw_bs[L][slot], 16)

                for pair in range(4):
                    load(None, pair)
                with sp.Fori(0, 2) as it:
                    load(it, 4)
                    load(it, 5)
                if L == 0:
                    sp.dma_start(w2_a[:, :, :].rearrange("p a d -> p (a d)"), w2t).then_inc(s_w2, 16)
                load(None, 8)
                load(None, 9)
                rest = WA_FFN - WA[L]
                sp.wait_ge(s["a"], 32)
                sp.dma_start(raw_a[:, 0, 0:rest], wax[L][0]).then_inc(raw_as[L][0], 16)
                if L == 0:
                    for h in range(2):
                        sp.wait_ge(s["b"], 28 + 4 * h)
                        sp.dma_start(raw_b[:, h, :], wdown0[h]).then_inc(raw_bs[0][h], 16)
                sp.wait_ge(ff[L]["w"], pieces_until(L, "a9"))
                sp.dma_start(raw_a[:, 1, 0:rest], wax[L][1]).then_inc(raw_as[L][1], 16)
            o_v = out.rearrange("(t p) d -> p t d", p=P)
            sp.wait_ge(ff[1]["xadd"], 8)
            sp.dma_start(o_v[:, 0:4, :], x[:, 0:4, :]).then_inc(s_out, 16)
            for t in range(4, 8):
                sp.wait_ge(ff[1]["xadd"], 8 + t + 1)
                sp.dma_start(o_v[:, t, :], x[:, t, :]).then_inc(s_out, 16)
            sp.wait_ge(s_out, 5 * 16)

        @block.gpsimd
        def _(pool):
            nc.gpsimd.memset(zero[:, :], 0.0).then_inc(s_zero, 1)
            nc.gpsimd.memset(neg_half[:, :], -0.5).then_inc(s_half, 1)
            pool.wait_ge(s_zero, 1)
            pool.wait_ge(s_half, 1)
            for t in range(4):
                ln_pool(pool, 0, t)
            pool.wait_ge(s_rope, 16)
            pool.wait_ge(s_scq, 1)
            for a in range(3):
                nc.gpsimd.tensor_tensor(cos_t[:, :, a, :], cos_c, scl[:, a // 2, :].unsqueeze(1).broadcast_to([P, 2, DH]),
                                        ALU.mult).then_inc(s_tab, 1)
            for t in range(4, TILES):
                ln_pool(pool, 0, t)
            slots(pool, 0, pool_slot, lambda c: None, pool_tail(pool, 0))
            for n in range(4, len(pieces[0])):
                pool_piece(pool, 0, n)
            pool_lo(pool, 0)
            pool_lo(pool, 1)
            pool.wait_ge(raw_as[1][0], 16)
            pool.wait_ge(ff[0]["up"], 12)
            w = WA[1] // 4
            for part in range(4):
                cs = slice(part * w, (part + 1) * w)
                split(a_w[0][0][:, cs], a_w[0][1][:, cs], raw_a[:, 0, cs], pool, at[1]["a0hi"],
                      lambda: pool.wait_ge(at[1]["a0hi"], part + 1), at[1]["a0"])
                if part == 1:
                    for t in range(4):
                        ln_pool(pool, 2, t)
                    pool_lo(pool, 2)
            pool_lo(pool, 3)
            slots(pool, 1, pool_slot, pool_head, pool_tail(pool, 1))
            for n in range(4, len(pieces[1])):
                pool_piece(pool, 1, n)

        QA = WA[0] // 4

        @block.scalar
        def _(act):
            act.dma_start(cst[:, 0:256], consts[:, 0:256]).then_inc(s_ident, 16)
            act.dma_start(raw_a[:, 0, 0:WA[0]], wa[0][0]).then_inc(raw_as[0][0], 16)
            act.dma_start(scl[:, :, :], scales).then_inc(s_scl, 16)
            act.dma_start(cst[:, 256:768], consts[:, 256:768]).then_inc(s_rope, 16)
            act.dma_start(cst[:, 768:1536], consts[:, 768:1536]).then_inc(s_mask, 16)
            act.wait_ge(raw_as[0][0], 16)
            nc.scalar.copy(a_w[0][0][:, 0:WA[0]], raw_a[:, 0, 0:WA[0]]).then_inc(at[0]["a0hi"], 1)
            for t in range(4):
                ln_act(act, 0, t, 4 + t)
            act.wait_ge(raw_as[0][1], 16)
            for part in range(4):
                cs = slice(part * QA, (part + 1) * QA)
                nc.scalar.copy(a_w[1][0][:, cs], raw_a[:, 1, cs]).then_inc(at[0]["ahi"], 1)
            for L in range(2):
                def head(c):
                    if L == 0 and -4 <= c < 0:
                        ln_act(act, 0, c + 8, 6 + c % 2)
                    elif L == 1 and c == -3:
                        act_hi(act, 0, 3)
                    elif L == 1 and c == -2:
                        for t in range(4, 8):
                            ln_act(act, 2, t, LN2_BANK[t])

                def tail(t):
                    if 2 <= t < 6:
                        if t == 2:
                            act.wait_ge(at[L]["proj"], UNITS)
                            if L == 1:
                                act.wait_ge(at[L]["vproj"], UNITS)
                        ln_act(act, 2 * L + 1, t - 2, PJ_BANK + t % 2)
                    if L == 1 and 1 <= t < 5:
                        act_hadamard(act, t - 1)

                slots(act, L, act_slot, head, tail)
                (act_ffn0, act_ffn1)[L](act)

        @block.vector
        def _(dve):
            for t in (0, 2):
                dve.wait_ge(s_x[t // 2], 16)
                ln_dve_stats(dve, 0, t, t + 1)
            for t in range(4):
                ln_dve_scale(dve, 0, t)
            dve.wait_ge(at[0]["a0hi"], 1)
            nc.vector.tensor_tensor(a_w[0][1][:, 0:WA[0]], raw_a[:, 0, 0:WA[0]], a_w[0][0][:, 0:WA[0]].bitcast(F32),
                                    ALU.subtract).then_inc(at[0]["a0"], 1)
            dve.wait_ge(s_scl, 16)
            nc.vector.tensor_scalar(scl[:, 0::2, :], scl[:, 0::2, :], ATTN_SCALE, None, ALU.mult).then_inc(s_scq, 1)
            for t in range(4):
                ln_dve_lo(dve, 0, t, 4 + t)
            dve.wait_ge(s_rope, 16)
            dve.wait_ge(s_scq, 1)
            for a in range(3):
                nc.vector.tensor_tensor(sin_t[:, :, a, :], sin_c, scl[:, 2 + a // 2, :].unsqueeze(1).broadcast_to([P, 2, DH]),
                                        ALU.mult).then_inc(s_tab, 1)
            for t in (4, 6):
                dve.wait_ge(s_x[t // 2], 16)
                ln_dve_stats(dve, 0, t, t + 1)
            ln_dve_scale(dve, 0, 4)
            ln_dve_scale(dve, 0, 5)
            dve.wait_ge(s_tab, 6)
            dve.wait_ge(s_mask, 16)
            for L in range(2):
                def tail(t):
                    st = 2 * L + 1
                    if 0 <= t:
                        dve.wait_ge(at[L]["opadd"], UNITS - 8 + t + 1)
                        ln_dve_bn(dve, st, t)
                    if 1 <= t:
                        ln_dve_scale(dve, st, t - 1)
                    if 0 <= t:
                        ln_dve_aggr(dve, st, t)
                    if 2 <= t < 6:
                        ln_dve_lo(dve, st, t - 2, PJ_BANK + t % 2)
                    if 0 <= t:
                        ln_dve_ve(dve, st, t)

                def head(c):
                    if L == 0 and -4 <= c < 0:
                        if c < -2:
                            ln_dve_scale(dve, 0, c + 10)
                        ln_dve_lo(dve, 0, c + 8, 6 + c % 2)
                    if L == 0 and -3 <= c < 1:
                        cs = slice((c + 3) * QA, (c + 4) * QA)
                        dve.wait_ge(at[0]["ahi"], c + 4)
                        nc.vector.tensor_tensor(a_w[1][1][:, cs], raw_a[:, 1, cs], a_w[1][0][:, cs].bitcast(F32),
                                                ALU.subtract).then_inc(at[0]["a"], 1)
                    if L == 1 and c == -4:
                        dve_count(dve, 3, 1)
                        dve_keep(dve, 3, (0, 1))
                    elif L == 1 and c == -3:
                        dve_keep(dve, 3, (2, 3))
                        dve_lo23(dve, 3)
                    elif L == 1 and c == -2:
                        for tt in (0, 2):
                            dve_xadd(dve, 0, 3, tt)
                            dve_xadd(dve, 0, 3, tt + 1)
                            dve.wait_ge(ff[0]["xadd"], 12 + tt + 2)
                            ln_dve_stats(dve, 2, 4 + tt, 5 + tt)
                        for t in range(4, 8):
                            ln_dve_scale(dve, 2, t)
                        for t in range(4, 8):
                            ln_dve_lo(dve, 2, t, LN2_BANK[t])

                slots(dve, L, dve_slot, head, tail)
                (dve_ffn0, dve_ffn1)[L](dve)

        @block.tensor
        def _(pe):
            pe.wait_ge(s_ident, 16)
            for t in range(4):
                ln_pe(pe, 0, t, 4 + t)
            for L in range(2):
                def head(c):
                    if L == 0 and -4 <= c < 0:
                        pe.wait_ge(ln["lo"], max(4, c + 7))
                        ln_pe(pe, 0, c + 8, 6 + c % 2)
                    elif L == 1 and c == -3:
                        pe_last_down(pe, 0)
                    elif L == 1 and c == -2:
                        for t in range(4, 8):
                            pe.wait_ge(ff[0]["xadd"], 12 + t - 3)
                            ln_pe(pe, 2, t, LN2_BANK[t])

                def tail(t):
                    if L == 1 and 1 <= t < 5:
                        pe_hadamard(pe, t - 1)
                    if 1 <= t < 5:
                        if t == 1:
                            pe.wait_ge(at[L]["rot" if L == 0 else "qkev"], UNITS)
                        elif t >= 3:
                            pe.wait_ge(ln["lo"], 8 * (2 * L + 1) + t - 2)
                        ln_pe(pe, 2 * L + 1, t - 1, PJ_BANK + (t - 1) % 2)

                slots(pe, L, pe_slot, head, tail)
                (pe_ffn0, pe_ffn1)[L](pe)


def shape_constants(np):
    i = np.arange(P)
    ident = np.eye(P, dtype=np.float32)
    had = np.ones((1, 1), np.float32)
    while had.shape[0] < P:
        had = np.block([[had, had], [had, -had]])
    past, window = i[None, :] <= i[:, None], i[None, :] > i[:, None]
    low = np.float32(MASKED)
    tri = np.where(past, np.float32(0), low)
    win = np.where(window, np.float32(0), low)
    mask0 = np.concatenate([tri, win, tri], 1)
    mask1 = np.concatenate([tri, np.zeros((P, P)), tri], 1)
    frac = np.arange(0, DH, 2, dtype=np.float32) / np.float32(DH)
    timescale = (np.float32(ROPE_BASE) ** frac).astype(np.float32)
    angle = np.arange(2 * P, dtype=np.float32)[:, None] / timescale
    cos, sin = np.cos(angle.astype(np.float64)), np.sin(angle.astype(np.float64))
    cos = np.concatenate([cos, cos], 1).reshape(2, P, DH).transpose(1, 0, 2).reshape(P, 2 * DH)
    sin = np.concatenate([-sin, sin], 1).reshape(2, P, DH).transpose(1, 0, 2).reshape(P, 2 * DH)
    return np.concatenate([ident, had, cos, sin, mask0, mask1], 1).astype(np.float32)


def kernel(**inputs):
    import numpy as np
    import concourse.bacc as bacc
    from concourse.bass_utils import run_bass_kernel_spmd

    a = {n: np.asarray(v) for n, v in inputs.items()}

    def rows(w):
        return w.reshape(NC, P, -1).transpose(1, 0, 2)

    q, kv = a["L0_attn_q_kernel"], a["L0_attn_kv_kernel"]
    pairs0 = [rows(np.concatenate([q[2 * p], q[2 * p + 1], kv[0, p], kv[1, p]], 1)).reshape(P, -1) for p in range(PAIRS)]
    wq, wk, wv = (a[f"L1_attn_W_{n}"].transpose(0, 2, 1) for n in "QKV")
    pairs1 = [rows(np.concatenate([wq[2 * p], wk[2 * p], wq[2 * p + 1], wk[2 * p + 1], wv[2 * p], wv[2 * p + 1]], 1))
              .reshape(P, -1) for p in range(PAIRS)]
    def by_four(w):
        return w.reshape(D, 2, P, 4).transpose(0, 1, 3, 2).reshape(D, 2, 4 * P)

    g0, u0 = by_four(a["L0_ffn_w_gate"]), by_four(a["L0_ffn_w_up"])
    g1, u1 = (a[f"L1_ffn_W{n}"].T.reshape(D, 2, 4 * P) for n in (1, 3))
    halves = [[rows(np.concatenate([g[:, t], u[:, t]], 1)).reshape(P, -1) for t in range(2)] for g, u in ((g0, u0), (g1, u1))]
    wa = [np.stack([w[:, :WA[L]] for w in (pairs0, pairs1)[L] + halves[L]]) for L in range(2)]
    wax = [np.stack([w[:, WA[L]:] for w in halves[L]]) for L in range(2)]
    wb0 = a["L0_attn_out_kernel"].reshape(PAIRS, 2, DH, D).transpose(0, 2, 1, 3).reshape(PAIRS, P, -1)
    wb1 = a["L1_attn_W_O"].T.reshape(PAIRS, 2, DH, D).transpose(0, 2, 1, 3).reshape(PAIRS, P, -1)
    down0 = a["L0_ffn_w_down"].reshape(2, P, 4 * D)
    w2t = a["L1_ffn_W2"].T.reshape(8, P, D).transpose(1, 0, 2).reshape(P, -1)
    sq, sk = a["L0_attn_q_norm_scale"], a["L0_attn_k_norm_scale"]
    swap = np.roll(np.arange(DH), DH // 2)
    scales = np.broadcast_to(np.stack([sq, sk, sq[swap], sk[swap]])[None], (P, 4, DH))
    arrays = {
        "x": a["L0_attn_x"].reshape(TOK, D), "wa0": wa[0], "wa1": wa[1], "wax0": wax[0], "wax1": wax[1],
        "wb0": wb0, "wb1": wb1, "wdown0": down0, "w2t": w2t, "consts": shape_constants(np), "scales": scales,
    }
    arrays = {n: np.ascontiguousarray(v) for n, v in arrays.items()}
    nc = bacc.Bacc("TRN2", target_bir_lowering=False, num_devices=1)
    d = {n: nc.dram_tensor(f"in_{n}", v.shape, F32, kind="ExternalInput").ap() for n, v in arrays.items()}
    out = nc.dram_tensor("out", (TOK, D), F32, kind="ExternalOutput").ap()
    build(nc, d["x"], (d["wa0"], d["wa1"]), (d["wax0"], d["wax1"]), (d["wb0"], d["wb1"]), d["wdown0"], d["w2t"],
          d["consts"], d["scales"], out)
    r = run_bass_kernel_spmd(nc, [{f"in_{n}": v for n, v in arrays.items()}], core_ids=[0])
    return r.results[0]["out"].reshape(4, 256, D)
```
